# Optimizing a Trainium2 kernel written in Bass

```python
import numpy as np
import jax
import jax.numpy as jnp

def _softmax(x, axis=-1):
    return jax.nn.softmax(x, axis=axis)

def _gelu(x):
    return jax.nn.gelu(x, approximate=True)

def _silu(x):
    return jax.nn.silu(x)

def _sigmoid(x):
    return jax.nn.sigmoid(x)

def _layernorm(x, axis=-1, eps=1e-05):
    m = jnp.mean(x, axis=axis, keepdims=True)
    v = jnp.var(x, axis=axis, keepdims=True)
    return (x - m) / jnp.sqrt(v + eps)

def _scatter_add(tgt, idx, src, axis=0):
    return tgt.at[idx].add(src)

def _segment_sum(src, seg, n):
    return jax.ops.segment_sum(src, seg, n)
kernel_name = 'mk_adj_ffn_d1_adj_r2_ca9358'

def setup_inputs(seed: int=0):
    np.random.seed(seed)
    _w = jnp.asarray

    def _rec_inputs():
        import jax
        import jax.numpy as jnp
        _gk = jax.random.key(seed)
        x = -0.0002928 + 1 * jax.random.normal(jax.random.fold_in(_gk, 1), (64, 128, 128), jnp.float32)
        _w = (1.0 + jnp.arange(128, dtype=jnp.float32)) ** (-0.5)
        _w = _w / _w.mean()
        _pij = jnp.clip(0.015625 * _w[:, None] * _w[None, :], 0.0, 1.0)
        _a = jax.random.uniform(jax.random.fold_in(_gk, 2), (64, 128, 128)) < _pij
        _af = _a.astype(jnp.float32)
        adj = _af
        return (x, adj)
    x, adj = _rec_inputs()

    def _L0_gnn_setup():
        import jax, jax.numpy as jnp
        import numpy as np
        ALPHA = 0.2
        NEG = -9000000000000000.0
        key = jax.random.key(seed)
        k1, k2, k3, k4 = jax.random.split(key, 4)
        B, N, F_in, F_out = (8, 1024, 128, 128)
        x = jax.random.normal(k1, (B, N, F_in), dtype=jnp.float32)
        adj = (jax.random.uniform(k2, (B, N, N)) < 0.05).astype(jnp.float32)
        W = jax.random.normal(k3, (F_in, F_out), jnp.float32) * (1.414 * np.sqrt(2.0 / (F_in + F_out)))
        a = jax.random.normal(k4, (2 * F_out, 1), jnp.float32) * (1.414 * np.sqrt(2.0 / (2 * F_out + 1)))
        return {'input': x, 'adj': adj, 'W': W, 'a': a}
    _L0_gnn_all = _L0_gnn_setup()
    _L0_gnn_in = {k: v for k, v in _L0_gnn_all.items() if k in ('W', 'a')}
    del _L0_gnn_all

    def _L0_ffn_setup():
        import jax, jax.numpy as jnp
        import numpy as np
        TOP_K = 2
        key = jax.random.key(seed)
        ks = jax.random.split(key, 4)
        B, L, D, H, E = (8, 2048, 128, 512, 8)
        s = 0.02
        return {'x': jax.random.normal(ks[0], (B, L, D), jnp.float32), 'Wg': jax.random.normal(ks[1], (D, E), jnp.float32) * s, 'bg': jnp.zeros((E,), jnp.float32), 'W1': jax.random.normal(ks[2], (E, D, H), jnp.float32) * s, 'b1': jnp.zeros((E, H), jnp.float32), 'W2': jax.random.normal(ks[3], (E, H, D), jnp.float32) * s, 'b2': jnp.zeros((E, D), jnp.float32)}
    _L0_ffn_all = _L0_ffn_setup()
    _L0_ffn_in = {k: v for k, v in _L0_ffn_all.items() if k in ('Wg', 'bg', 'W1', 'b1', 'W2', 'b2')}
    del _L0_ffn_all
    return {'x': x, 'adj': adj, 'L0_gnn_W': _L0_gnn_in['W'], 'L0_gnn_a': _L0_gnn_in['a'], 'L0_ffn_Wg': _L0_ffn_in['Wg'], 'L0_ffn_bg': _L0_ffn_in['bg'], 'L0_ffn_W1': _L0_ffn_in['W1'], 'L0_ffn_b1': _L0_ffn_in['b1'], 'L0_ffn_W2': _L0_ffn_in['W2'], 'L0_ffn_b2': _L0_ffn_in['b2']}

def reference(x, adj, L0_gnn_W, L0_gnn_a, L0_ffn_Wg, L0_ffn_bg, L0_ffn_W1, L0_ffn_b1, L0_ffn_W2, L0_ffn_b2):
    import jax
    import jax.numpy as jnp

    def _L0_gnn_ref(input, adj, W, a):
        import jax, jax.numpy as jnp
        import numpy as np
        ALPHA = 0.2
        NEG = -9000000000000000.0
        F_out = W.shape[1]
        h = input @ W
        a1 = a[:F_out, 0]
        a2 = a[F_out:, 0]
        s = jnp.einsum('bnf,f->bn', h, a1 + a2)
        e = jax.nn.leaky_relu(s, ALPHA)[:, :, None]
        logits = jnp.where(adj > 0, e, NEG)
        att = jax.nn.softmax(logits, axis=2)
        h_prime = jnp.einsum('bij,bjf->bif', att, h)
        return jax.nn.elu(h_prime)

    def _L0_ffn_ref(x, Wg, bg, W1, b1, W2, b2):
        import jax, jax.numpy as jnp
        import numpy as np
        TOP_K = 2
        B, L, D = x.shape
        E = W1.shape[0]
        xf = x.reshape(-1, D)
        gate_logits = xf @ Wg + bg
        top_w, top_i = jax.lax.top_k(gate_logits, TOP_K)
        top_w = jax.nn.softmax(top_w, axis=-1)
        w_dense = jnp.sum(jax.nn.one_hot(top_i, E, dtype=xf.dtype) * top_w[..., None], axis=1)
        out = jnp.zeros_like(xf)
        for e in range(E):
            h = jax.nn.gelu(xf @ W1[e] + b1[e], approximate=False)
            out = out + w_dense[:, e:e + 1] * (h @ W2[e] + b2[e])
        return out.reshape(B, L, D)
    x = x + _L0_gnn_ref(_layernorm(x, axis=-1), adj, L0_gnn_W, L0_gnn_a)
    x = x + _L0_ffn_ref(_layernorm(x, axis=-1), L0_ffn_Wg, L0_ffn_bg, L0_ffn_W1, L0_ffn_b1, L0_ffn_W2, L0_ffn_b2)
    return x

_drawn_inputs = setup_inputs


def setup_inputs(seed=0):
    import zlib

    import numpy as np

    out = dict(_drawn_inputs(seed))
    spreads = {'L0_ffn_bg': (0.0, 0.1), 'L0_ffn_b1': (0.0, 0.595), 'L0_ffn_b2': (0.0, 0.1)}
    factors = {}
    for name, (base, spread) in spreads.items():
        noise = np.random.default_rng([zlib.crc32(name.encode()), seed]).standard_normal(out[name].shape)
        drawn = base * np.exp(spread * noise) if base else spread * noise
        out[name] = jnp.asarray(drawn.astype(out[name].dtype))
    for name, factor in factors.items():
        out[name] = (out[name] * factor).astype(out[name].dtype)
    return out
```

```python
from contextlib import ExitStack

import concourse.bass as bass
from concourse import mybir

ALU = mybir.AluOpType
ACT = mybir.ActivationFunctionType
AX = mybir.AxisListType
F32 = mybir.dt.float32
F32R = mybir.dt.float32r
BF16 = mybir.dt.bfloat16
I32 = mybir.dt.int32

P = 128
ALPHA = 0.2
NEG = -9000000000000000.0
EPS = 1e-5
LOW = -3.0e38


def gat_moe(nc, x, adj, W, a, Wg, bg, W1, b1, W2, b2, out):
    B, N, D = x.shape
    E, _, H = W1.shape
    T = B * N
    G = 4
    NB = B // G
    C = H // P
    K = 2
    SLOTS = -(-(T * K // P + E - 1) // 4) * 4
    assert N == P and D == P and K * B == P and B % (2 * G) == 0 and SLOTS <= 256 and B * (K + 1) <= 256

    x_dram = x.rearrange("(b g) n d -> b n g d", g=G)
    adj_dram = adj.rearrange("(b g) n d -> b n g d", g=G)
    out_dram = out.rearrange("(b g) n d -> b n g d", g=G)

    with ExitStack() as ctx:
        def sb(name, shape, dt=F32):
            return ctx.enter_context(nc.sbuf_tensor(name, shape, dt))

        def sem(name):
            return ctx.enter_context(nc.semaphore(name))

        tok_dram = nc.dram_tensor("tok_dram", (T, D), F32, kind="Internal").ap()
        y_dram = nc.dram_tensor("y_dram", (K * T + SLOTS * P, D), F32, kind="Internal").ap()
        b_dram = nc.dram_tensor("b_dram", (2, E * (H + D)), F32R, kind="Internal").ap()
        tok_store = tok_dram.rearrange("(b g n) d -> b n g d", g=G, n=N)
        y_load = y_dram[0:K * T, :].rearrange("(k b g n) d -> k b n g d", k=K, g=G, n=N)

        bank = [ctx.enter_context(nc.psum_tensor(f"bank{i}", [P, 512], F32)) for i in range(8)]

        ident = sb("ident", [P, P])
        ones = sb("ones", [P, P])
        lower = sb("lower", [P, P])
        ones_r = sb("ones_r", [2, P], F32R)
        w_gat = sb("w_gat", [P, D])
        w_gatT = sb("w_gatT", [D, P])
        a_both = sb("a_both", [D, 2])
        a_sum = sb("a_sum", [D, 1])
        w_score = sb("w_score", [P, 1])
        w_gate = sb("w_gate", [P, E])
        b_gate = sb("b_gate", [P, E])
        HALF = H // 2
        w_raw = sb("w_raw", [P, 2, 2, HALF])
        w1_hi = sb("w1_hi", [P, E, H], F32R)
        w1_lo = sb("w1_lo", [P, E, H], F32R)
        w2_hl = sb("w2_hl", [P, E, C, 2, D], F32R)
        BR = E * (H + D) // P
        b_raw = sb("b_raw", [BR, P])
        b_high = sb("b_high", [BR, P], F32R)
        b_low = sb("b_low", [BR, P], F32R)
        b_hl = sb("b_hl", [2, E * (H + D)], F32R)
        b1_hl = b_hl[:, 0:E * H].rearrange("p (e h) -> p e h", e=E)
        b2_hl = b_hl[:, E * H:E * (H + D)].rearrange("p (e d) -> p e d", e=E)

        x_all = sb("x_all", [P, B, D])
        x_ring = sb("x_ring", [P, 2, G, D])
        x2_ring = sb("x2_ring", [P, 2, G, D])
        adj_ring = sb("adj_ring", [P, 2, G, N])
        mask = sb("mask", [P, 2, G, N])
        stats = sb("stats", [P, G, 6])
        mv = sb("mv", [P, 2, G, 2])
        rstd = sb("rstd", [P, 2, G])
        stats2 = sb("stats2", [P, G, 6])
        mv2 = sb("mv2", [P, G, 2])
        rstd2 = sb("rstd2", [P, G])
        half = sb("half", [P, G])
        minus1 = sb("minus1", [P, G])
        xn = sb("xn", [P, 2, G, D])
        xnT = sb("xnT", [P, G, N])
        h_sb = sb("h_sb", [P, 2, G, D])
        count = sb("count", [P, 2, G])
        score = sb("score", [P, 2, G])
        tiny = sb("tiny", [P, 16, G])
        shift = sb("shift", [P, 2, G])
        expo = sb("expo", [P, 2, G])
        att_a = sb("att_a", [P, 2, G])
        att_b = sb("att_b", [P, 2, G])
        act_h = sb("act_h", [P, 2, H])
        att = act_h[:, 0, :].rearrange("p (g n) -> p g n", g=G)
        attT = act_h[:, 1, :].rearrange("p (g n) -> p g n", g=G)
        exp_u = sb("exp_u", [P, G, D])
        xe = sb("xe", [P, G, D])
        xn2 = sb("xn2", [P, 2, G, D])
        xn2T = sb("xn2T", [P, G, N])
        logits = sb("logits", [P, B, E])


        GROUPS = K * B
        rev = sb("rev", [P, E])
        iota_i = sb("iota_i", [P, 2 * P + SLOTS], I32)
        rev_i = sb("rev_i", [P, E], I32)
        node_i = sb("node_i", [P, 1], I32)
        slot_i = sb("slot_i", [P, SLOTS], I32)
        iota_q = sb("iota_q", [P, P], BF16)
        iota_s = sb("iota_s", [P, SLOTS], BF16)
        iota_sf = sb("iota_sf", [1, SLOTS])
        code = sb("code", [P, GROUPS])
        node = sb("node", [P, 1])
        pad_row = sb("pad_row", [P, SLOTS])
        reset = sb("reset", [P, E, B])
        first = sb("first", [P, 2, B])
        work = [t[:].rearrange("p g n -> p (g n)").rearrange("p (b e) -> p b e", b=B) for t in (xnT, xn2T)]
        key = sb("key", [P, K, B])
        chosen = xn[:].rearrange("p k g d -> p (k g d)").rearrange("p (k b e) -> p k b e", k=K, b=B)
        member = sb("member", [P, E, B])
        upto = sb("upto", [P, E, B])
        rows = sb("rows", [P, 6, E])
        rows_i = sb("rows_i", [P, 2, E], I32)
        pos = sb("pos", [P, GROUPS])
        pos_i = sb("pos_i", [P, 3, GROUPS], I32)
        pos_q = sb("pos_q", [P, GROUPS])
        pos_s = sb("pos_s", [P, GROUPS])
        gap = sb("gap", [P, B])
        gate = sb("gate", [P, K, B])
        past = h_sb[0:1].rearrange("p k g d -> p (k g d)")[:, 0:(E - 1) * SLOTS].rearrange("p (e s) -> p e s", e=E - 1)
        slot_e = sb("slot_e", [1, SLOTS])
        slot_expert = sb("slot_expert", [1, SLOTS], I32)
        RING = 8
        pos_now, code_now = sb("pos_now", [P, RING]), sb("code_now", [P, RING])
        hot_q = sb("hot_q", [P, RING, P], BF16)
        hot_s = sb("hot_s", [P, RING, 2, SLOTS], BF16)
        found = sb("found", [P, 2, SLOTS])
        row = sb("row", [P, 4, SLOTS])
        gather_row = sb("gather_row", [P, SLOTS], I32)
        y_row = sb("y_row", [P, SLOTS], I32)

        gidx = [sb(f"gidx{i}", [P, 1], I32) for i in range(4)]
        yidx = [sb(f"yidx{i}", [P, 1], I32) for i in range(4)]
        xg = [xe[:, i, :] for i in range(4)]
        xg_hi = sb("xg_hi", [P, 2, P], F32R)
        xg_lo = sb("xg_lo", [P, 2, P], F32R)
        hT_hi = sb("hT_hi", [P, 2, H], F32R)
        hT_lo = sb("hT_lo", [P, 2, H], F32R)
        y_sb = [exp_u[:, i, :] for i in range(4)]
        y_in = [xn, h_sb]

        x_in = [sem(f"x_in{i}") for i in range(2)]
        ring_in = [sem(f"ring_in{i}") for i in range(2)]
        x2_kept = [sem(f"x2_kept{i}") for i in range(2)]
        adj_in = [sem(f"adj_in{i}") for i in range(2)]
        const_in, b_in = sem("const_in"), sem("b_in")
        w_in = [sem(f"w_in{i}") for i in range(4)]
        made, made_i, made_c = sem("made"), sem("made_i"), sem("made_c")
        a_summed, wT_done, wT_copied, ws_done, ws_copied = (
            sem("a_summed"), sem("wT_done"), sem("wT_copied"), sem("ws_done"), sem("ws_copied"))
        w_high, w_low = sem("w_high"), sem("w_low")
        b_parted = [sem(f"b_parted{i}") for i in range(2)]
        b_high_made, b_low_made, b_joined = sem("b_high_made"), sem("b_low_made"), sem("b_joined")
        stat_step, rstd_step, normed = sem("stat_step"), sem("rstd_step"), sem("normed")
        xT_done, xT_copied = sem("xT_done"), sem("xT_copied")
        h_done, h_copied = sem("h_done"), sem("h_copied")
        mask_made, counted, score_copied = sem("mask_made"), sem("counted"), sem("score_copied")
        soft_step, soft_exp, att_done = sem("soft_step"), sem("soft_exp"), sem("att_done")
        aT_done, aT_copied = sem("aT_done"), sem("aT_copied")
        u_done, u_exp, xe_step, x2_done = sem("u_done"), sem("u_exp"), sem("xe_step"), sem("x2_done")
        stat2_step, rstd2_step, normed2 = sem("stat2_step"), sem("rstd2_step"), sem("normed2")
        x2T_done, x2T_copied = sem("x2T_done"), sem("x2T_copied")
        logit_done, logit_copied = sem("logit_done"), sem("logit_copied")
        tok_out = [sem(f"tok_out{i}") for i in range(2)]
        tokens_stored = sem("tokens_stored")
        route = sem("route")
        totals, counts = sem("totals"), sem("counts")
        gap_made, gap_exp, gate_step = sem("gap_made"), sem("gap_exp"), sem("gate_step")
        pos_made = sem("pos_made")
        hot_dve, hot_pool, hot_used = sem("hot_dve"), sem("hot_pool"), sem("hot_used")
        now_set = sem("now_set")
        found_copied = sem("found_copied")
        experts_known = sem("experts_known")
        gidx_set, yidx_set = sem("gidx_set"), sem("yidx_set")
        gathered = [sem(f"gathered{i}") for i in range(4)]
        scattered = [sem(f"scattered{i}") for i in range(4)]
        gT_done, gT_high, gT_low = sem("gT_done"), sem("gT_high"), sem("gT_low")
        pre_done, gelu_done = sem("pre_done"), sem("gelu_done")
        hT_done, hT_high, hT_low_done = sem("hT_done"), sem("hT_high"), sem("hT_low_done")
        y_done, y_copied = sem("y_done"), sem("y_copied")
        y0_in = [sem(f"y0_in{i}") for i in range(2)]
        y1_in = [sem(f"y1_in{i}") for i in range(2)]
        first_added, both_added = sem("first_added"), sem("both_added")
        out_sent = [sem(f"out_sent{i}") for i in range(2)]

        SOFT = 25

        def attention_steps(eng, step):
            def at(i):
                step(i // 2, i % 2, lambda k: 0 <= i - k < NB)
            for i in range(6):
                at(i)
            with eng.Fori(3, NB // 2) as q:
                for r in range(2):
                    step(q, r, lambda k: True)
            for i in range(NB, NB + 6):
                at(i)

        def batch(q, r, k):
            e = (r - k) % 2
            turn = q + (r - k - e) // 2
            return turn * 2 + e, e, turn

        def slot_steps(eng, step):
            def at(i):
                step(i // 4, i % 4, lambda k: 0 <= i - k < SLOTS)
            for i in range(8):
                at(i)
            with eng.Fori(2, SLOTS // 4) as q:
                for r in range(4):
                    step(q, r, lambda k: True)
            for i in range(SLOTS, SLOTS + 7):
                at(i)

        def slot(q, r, k):
            e = (r - k) % 4
            turn = q + (r - k - e) // 4
            return turn * 4 + e, e, turn

        def hot_steps(eng, step):
            for r in range(RING):
                step(0, r, r == 0, False)
            with eng.Fori(1, GROUPS // RING - 1) as q:
                for r in range(RING):
                    step(q, r, False, False)
            for r in range(RING):
                step(GROUPS // RING - 1, r, False, r == RING - 1)

        def wait(eng, semaphore, value):
            if not isinstance(value, int) or value > 0:
                eng.wait_ge(semaphore, value)

        def expert_of(t, e):
            return t[bass.ds(e, 1)].rearrange("o a b -> (o a) b")

        def one(t, e):
            v = t[:, bass.ds(e, 1)]
            return v.rearrange("p o h -> p (o h)") if len(v.shape) == 3 else v.rearrange("p o c k d -> p (o c) k d")

        def some(t, j):
            return t[:, bass.ds(j * G, G), :]

        def dram(t, j):
            return t[bass.ds(j, 1)].rearrange("o n g d -> (o n) g d")

        block = ctx.enter_context(nc.Block())

        @block.sync
        def _(sp):
            def load(q, r, has):
                if has(0):
                    j, e, turn = batch(q, r, 0)
                    wait(sp, normed, j - 1)
                    sp.dma_start(x_ring[:, e], dram(x_dram, j)).then_inc(ring_in[e], 16)
                    wait(sp, x_in[e], turn * 16)
                    sp.dma_start(some(x_all, j), dram(x_dram, j)).then_inc(x_in[e], 16)
                    wait(sp, mask_made, j - 1)
                    sp.dma_start(adj_ring[:, e], dram(adj_dram, j)).then_inc(adj_in[e], 16)
                if has(0):
                    wait(sp, w_low, j - 1)
                    sp.dma_start(w_raw[:, e, 0, :], expert_of(W1, turn)[:, e * HALF:(e + 1) * HALF]
                                 ).then_inc(w_in[e], 16)
                    sp.dma_start(w_raw[:, e, 1, :].rearrange("p (c d) -> p c d", d=D),
                                 expert_of(W2, turn).rearrange("(c p) d -> p c d", p=P)[:, e * C // 2:(e + 1) * C // 2, :]
                                 ).then_inc(w_in[2 + e], 16)
                if has(4):
                    j, e, turn = batch(q, r, 4)
                    sp.wait_ge(normed2, j + 1)
                    sp.dma_start(dram(tok_store, j), xn2[:, e]).then_inc(tok_out[e], 16)
                    sp.dma_start(some(x_all, j), x2_ring[:, e]).then_inc(x2_kept[e], 16)

            sp.dma_start(w_gat[:], W).then_inc(const_in, 16)
            for t in range(2):
                sp.dma_start(a_both[:, t:t + 1], a[t * D:(t + 1) * D, :]).then_inc(const_in, 16)
            sp.dma_start(w_gate[:], Wg).then_inc(const_in, 16)
            sp.dma_start(b_gate[:], bg.partition_broadcast(P)).then_inc(const_in, 16)
            attention_steps(sp, load)

            for e in range(2):
                sp.wait_ge(tok_out[e], 16 * NB // 2)
            sp.sem_inc(tokens_stored, 1)

            for e in range(4):
                sp.wait_ge(scattered[e], 16 * SLOTS // 4)
            def fetch(q, r):
                j = q * 2 + r
                wait(sp, both_added, j - 1)
                sp.dma_start(y_in[0][:, r], y_load[0, bass.ds(j, 1)].rearrange("o n g d -> (o n) g d")).then_inc(y0_in[r], 16)
                sp.dma_start(y_in[1][:, r], y_load[1, bass.ds(j, 1)].rearrange("o n g d -> (o n) g d")).then_inc(y1_in[r], 16)
            for r in range(2):
                fetch(0, r)
            with sp.Fori(1, NB // 2) as q:
                for r in range(2):
                    fetch(q, r)

        @block.gpsimd
        def _(pool):
            pool.memset(ident[:], 0.0)
            pool.memset(ones[:], 1.0)
            pool.memset(lower[:], 1.0)
            pool.memset(half[:], -0.5)
            pool.memset(minus1[:], -1.0)
            pool.memset(ones_r[:].bitcast(F32), 1.0)
            pool.memset(reset[:], 1.0)
            pool.iota(iota_i[:, 0:P], pattern=[[1, P]], base=0, channel_multiplier=0)
            pool.iota(iota_i[:, P:P + SLOTS], pattern=[[P, SLOTS]], base=K * T + B * P, channel_multiplier=1)
            pool.iota(iota_i[:, P + SLOTS:2 * P + SLOTS], pattern=[[1, P]], base=B, channel_multiplier=0).then_inc(made_i, 1)
            pool.wait_ge(made_i, 1)
            pool.affine_select(out=ident[:], in_=ident[:], compare_op=ALU.not_equal, fill=1.0, base=0,
                               pattern=[[-1, P]], channel_multiplier=1)
            pool.affine_select(out=lower[:], in_=lower[:], compare_op=ALU.is_ge, fill=0.0, base=-1,
                               pattern=[[1, P]], channel_multiplier=-1)
            pool.memset(reset[:, :, 0:1], 0.0)
            pool.iota(rev_i[:], pattern=[[-1, E]], base=E, channel_multiplier=0)
            pool.iota(node_i[:], pattern=[[1, 1]], base=0, channel_multiplier=1)
            pool.iota(slot_i[:], pattern=[[1, SLOTS]], base=0, channel_multiplier=0).then_inc(made, 1)
            pool.wait_ge(made, 1)
            for dst, src in ((iota_q[:], iota_i[:, 0:P]), (iota_s[:], slot_i[:]), (iota_sf[:], slot_i[0:1, :]),
                             (pad_row[:], iota_i[:, P:P + SLOTS]), (code[:], iota_i[:, P + SLOTS:2 * P + SLOTS]),
                             (rev[:], rev_i[:]), (node[:], node_i[:])):
                last = pool.tensor_copy(dst, src)
            last.then_inc(made_c, 1)

            def step(q, r, has):
                if has(0):
                    j, e, turn = batch(q, r, 0)
                    pool.wait_ge(stat_step, 2 * j + 2)
                    pool.nop(nofuse=True)
                    pool.tensor_scalar(tiny[:, 0, :], mv[:, e, :, 1], EPS, None, ALU.add).then_inc(rstd_step, 1)
                    pool.wait_ge(rstd_step, 2 * j + 1)
                    pool.nop(nofuse=True)
                    pool.tensor_tensor(rstd[:, e, :], tiny[:, 0, :], half[:], ALU.pow).then_inc(rstd_step, 1)
                if has(3):
                    j, e, turn = batch(q, r, 3)
                    pool.wait_ge(x_in[e], turn * 16 + 16)
                    pool.wait_ge(u_exp, j + 1)
                    wait(pool, x2_done, j)
                    pool.nop(nofuse=True)
                    pool.tensor_scalar(xe[:], exp_u[:], 1.0, -1.0, ALU.min, ALU.add).then_inc(xe_step, 1)
                    pool.wait_ge(xe_step, 2 * j + 1)
                    pool.nop(nofuse=True)
                    pool.tensor_tensor(xe[:], xe[:], some(x_all, j), ALU.add).then_inc(xe_step, 1)
                if has(1):
                    j, e, turn = batch(q, r, 1)
                    softmax_rows(j, e)
                if has(3):
                    j, e, turn = batch(q, r, 3)
                    pool.wait_ge(stat2_step, 2 * j + 2)
                    pool.nop(nofuse=True)
                    pool.tensor_scalar(tiny[:, 1, :], mv2[:, :, 1], EPS, None, ALU.add).then_inc(rstd2_step, 1)
                    pool.wait_ge(rstd2_step, 2 * j + 1)
                    pool.nop(nofuse=True)
                    pool.tensor_tensor(rstd2[:], tiny[:, 1, :], half[:], ALU.pow).then_inc(rstd2_step, 1)
                if has(0):
                    j, e, turn = batch(q, r, 0)
                    pool.wait_ge(adj_in[e], turn * 16 + 16)
                    wait(pool, att_done, j - 1)
                    pool.nop(nofuse=True)
                    pool.tensor_scalar(mask[:, e], adj_ring[:, e], 0.0, None, ALU.is_gt).then_inc(mask_made, 1)
                if has(0):
                    j, e, turn = batch(q, r, 0)
                    pool.wait_ge(w_high, j + 1)
                    pool.nop(nofuse=True)
                    w1_part = slice(e * HALF, (e + 1) * HALF)
                    w2_part = slice(e * C // 2, (e + 1) * C // 2)
                    pool.tensor_tensor(one(w1_lo, turn)[:, w1_part], w_raw[:, e, 0, :],
                                       one(w1_hi, turn)[:, w1_part].bitcast(F32), ALU.subtract)
                    pool.tensor_tensor(one(w2_hl, turn)[:, w2_part, 1, :], w_raw[:, e, 1, :].rearrange("p (c d) -> p c d", d=D),
                                       one(w2_hl, turn)[:, w2_part, 0, :].bitcast(F32), ALU.subtract).then_inc(w_low, 1)

            def softmax_rows(j, r):
                pool.wait_ge(score_copied, j + 1)
                pool.wait_ge(counted, j + 1)
                pool.nop(nofuse=True)
                s, c = score[:, r, :], count[:, r, :]
                t = [tiny[:, k, :] for k in range(2, 16)]
                e_, any_, full, m = t[0], t[1], t[2], t[3]
                ops = [
                    lambda: pool.tensor_scalar(t[4], s, 0.0, None, ALU.max),
                    lambda: pool.tensor_scalar(t[5], s, 0.0, ALPHA, ALU.min, ALU.mult),
                    lambda: pool.tensor_scalar(any_, c, 0.0, None, ALU.is_gt),
                    lambda: pool.tensor_scalar(full, c, float(N), None, ALU.is_ge),
                    lambda: pool.tensor_scalar(t[6], c, float(N), None, ALU.is_lt),
                    lambda: pool.tensor_tensor(e_, t[4], t[5], ALU.add),
                    lambda: pool.tensor_scalar(t[7], any_, -NEG, NEG, ALU.mult, ALU.add),
                    lambda: pool.tensor_scalar(t[8], e_, NEG, None, ALU.max),
                    lambda: pool.tensor_tensor(t[9], e_, full, ALU.mult),
                    lambda: pool.tensor_tensor(t[10], t[8], t[6], ALU.mult),
                    lambda: pool.tensor_tensor(t[9], t[9], t[10], ALU.add),
                    lambda: pool.tensor_tensor(t[9], t[9], any_, ALU.mult),
                    lambda: pool.tensor_tensor(m, t[9], t[7], ALU.add),
                    lambda: pool.tensor_tensor(t[11], e_, m, ALU.subtract),
                    lambda: pool.tensor_scalar(t[12], m, -1.0, NEG, ALU.mult, ALU.add),
                    lambda: pool.tensor_scalar(shift[:, 0, :], t[11], 0.0, None, ALU.min),
                    lambda: pool.tensor_scalar(shift[:, 1, :], t[12], 0.0, None, ALU.min),
                ]
                for n, op in enumerate(ops):
                    op().then_inc(soft_step, 1)
                    pool.wait_ge(soft_step, j * SOFT + n + 1)
                    pool.nop(nofuse=True)
                pool.tensor_scalar(t[4], c, -1.0, float(N), ALU.mult, ALU.add).then_inc(soft_step, 1)
                pool.wait_ge(soft_exp, j + 1)
                pool.wait_ge(soft_step, j * SOFT + 18)
                wait(pool, att_done, j - 1)
                pool.nop(nofuse=True)
                ops = [
                    lambda: pool.tensor_tensor(t[5], c, expo[:, 0, :], ALU.mult),
                    lambda: pool.tensor_tensor(t[6], t[4], expo[:, 1, :], ALU.mult),
                    lambda: pool.tensor_tensor(t[7], expo[:, 0, :], expo[:, 1, :], ALU.subtract),
                    lambda: pool.tensor_tensor(t[5], t[5], t[6], ALU.add),
                    lambda: pool.tensor_tensor(t[5], t[5], minus1[:], ALU.pow),
                    lambda: pool.tensor_tensor(att_a[:, r, :], t[7], t[5], ALU.mult),
                    lambda: pool.tensor_tensor(att_b[:, r, :], expo[:, 1, :], t[5], ALU.mult),
                ]
                for n, op in enumerate(ops):
                    op().then_inc(soft_step, 1)
                    pool.wait_ge(soft_step, j * SOFT + 19 + n)
                    pool.nop(nofuse=True)

            attention_steps(pool, step)

            pool.wait_ge(b_high_made, 1)
            pool.tensor_tensor(b_low[:], b_raw[:], b_high[:].bitcast(F32), ALU.subtract).then_inc(b_low_made, 1)
            pool.wait_ge(b_low_made, 1)
            pool.dma_start(b_dram[0].rearrange("(r p) -> r p", p=P), b_high[:]).then_inc(b_parted[0], 16)
            pool.dma_start(b_dram[1].rearrange("(r p) -> r p", p=P), b_low[:]).then_inc(b_parted[1], 16)
            pool.wait_ge(b_parted[0], 16)
            pool.wait_ge(b_parted[1], 16)
            pool.dma_start(b_hl[:], b_dram).then_inc(b_joined, 16)

            pool.wait_ge(pos_made, 1)

            def hot(q, r, first, last):
                n = q * RING + r
                if r == 0:
                    wait(pool, hot_pool, q * RING)
                    pool.tensor_copy(pos_now[:], pos_s[:, bass.ds(n, RING)])
                    pool.tensor_copy(code_now[:], code[:, bass.ds(n, RING)]).then_inc(now_set, 1)
                    pool.wait_ge(now_set, q + 1)
                wait(pool, hot_used, n - RING + 1)
                pool.nop(nofuse=True)
                pool.tensor_scalar(hot_s[:, r, 0, :], iota_s[:], pos_now[:, r:r + 1], code_now[:, r:r + 1],
                                   ALU.is_equal, ALU.mult).then_inc(hot_pool, 1)
            hot_steps(pool, hot)

            def step(q, r, has):
                if has(0):
                    j, e, turn = slot(q, r, 0)
                    pool.wait_ge(gidx_set, j + 1)
                    wait(pool, gT_done, j - 3)
                    pool.nop(nofuse=True)
                    pool.indirect_dma_start(xg[e], None, tok_dram, bass.IndirectOffsetOnAxis(ap=gidx[e][:], axis=0)
                                            ).then_inc(gathered[e], 16)
                if has(6):
                    j, e, turn = slot(q, r, 6)
                    pool.wait_ge(yidx_set, j + 1)
                    pool.wait_ge(y_copied, j + 1)
                    pool.nop(nofuse=True)
                    pool.indirect_dma_start(y_dram, bass.IndirectOffsetOnAxis(ap=yidx[e][:], axis=0), y_sb[e], None
                                            ).then_inc(scattered[e], 16)
            pool.wait_ge(tokens_stored, 1)
            slot_steps(pool, step)

        @block.scalar
        def _(act):
            b1_rows = b1.rearrange("e (c p) -> (e c) p", p=P)
            act.dma_start(b_raw[0:E * C, :], b1_rows).then_inc(b_in, 16)
            act.dma_start(b_raw[E * C:BR, :], b2).then_inc(b_in, 16)
            act.wait_ge(wT_done, 1)
            act.activation(w_gatT[:], bank[0][:, 0:P], ACT.Copy).then_inc(wT_copied, 1)
            act.wait_ge(ws_done, 1)
            act.activation(w_score[:], bank[1][:, 0:1], ACT.Copy).then_inc(ws_copied, 1)

            def step(q, r, has):
                if has(1):
                    j, e, turn = batch(q, r, 1)
                    act.wait_ge(xT_done, j + 1)
                    wait(act, h_done, j)
                    act.activation(xnT[:].rearrange("p g n -> p (g n)"), bank[0][:], ACT.Copy).then_inc(xT_copied, 1)
                if has(4):
                    j, e, turn = batch(q, r, 4)
                    act.wait_ge(x2T_done, j + 1)
                    wait(act, logit_done, j)
                    act.activation(xn2T[:].rearrange("p g n -> p (g n)"), bank[2][:], ACT.Copy).then_inc(x2T_copied, 1)
                if has(1):
                    j, e, turn = batch(q, r, 1)
                    act.wait_ge(h_done, j + 1)
                    wait(act, u_done, j - 1)
                    act.activation(h_sb[:, e].rearrange("p g d -> p (g d)"), bank[3 + e][:], ACT.Copy).then_inc(h_copied, 1)
                if has(0):
                    j, e, turn = batch(q, r, 0)
                    act.wait_ge(w_in[e], turn * 16 + 16)
                    act.activation(one(w1_hi, turn)[:, e * HALF:(e + 1) * HALF], w_raw[:, e, 0, :], ACT.Copy)
                    act.wait_ge(w_in[2 + e], turn * 16 + 16)
                    act.activation(one(w2_hl, turn)[:, e * C // 2:(e + 1) * C // 2, 0, :],
                                   w_raw[:, e, 1, :].rearrange("p (c d) -> p c d", d=D), ACT.Copy).then_inc(w_high, 1)
                if has(2):
                    j, e, turn = batch(q, r, 2)
                    act.wait_ge(aT_done, j + 1)
                    wait(act, u_done, j)
                    act.activation(attT.rearrange("p g n -> p (g n)"), bank[1][:], ACT.Copy).then_inc(aT_copied, 1)
                if has(2):
                    j, e, turn = batch(q, r, 2)
                    act.wait_ge(u_done, j + 1)
                    wait(act, xe_step, 2 * j - 1)
                    act.activation(exp_u[:].rearrange("p g d -> p (g d)"), bank[5 + e][:], ACT.Exp).then_inc(u_exp, 1)
                if has(1):
                    j, e, turn = batch(q, r, 1)
                    act.wait_ge(soft_step, j * SOFT + 17)
                    act.activation(expo[:], shift[:], ACT.Exp).then_inc(soft_exp, 1)

            attention_steps(act, step)

            act.wait_ge(b_in, 32)
            act.activation(b_high[:], b_raw[:], ACT.Copy).then_inc(b_high_made, 1)

            act.wait_ge(gap_made, 1)
            act.activation(gap[:], gap[:], ACT.Exp).then_inc(gap_exp, 1)
            act.wait_ge(hot_used, GROUPS)
            act.activation(found[:].rearrange("p a s -> p (a s)"), bank[0][:, 0:2 * SLOTS], ACT.Copy).then_inc(found_copied, 1)

            def step(q, r, has):
                if has(3):
                    j, e, turn = slot(q, r, 3)
                    act.wait_ge(gT_done, j + 1)
                    wait(act, pre_done, j - 1)
                    act.activation(xg_hi[:, e % 2], bank[e % 2][:, 0:P], ACT.Copy).then_inc(gT_high, 1)
                if has(4):
                    j, e, turn = slot(q, r, 4)
                    act.wait_ge(pre_done, j + 1)
                    wait(act, hT_done, j - 1)
                    act.activation(act_h[:, e % 2], bank[2 + e % 2][:], ACT.Gelu).then_inc(gelu_done, 1)
                if has(5):
                    j, e, turn = slot(q, r, 5)
                    act.wait_ge(hT_done, j + 1)
                    wait(act, y_done, j - 1)
                    act.activation(hT_hi[:, e % 2], bank[4 + e % 2][:], ACT.Copy).then_inc(hT_high, 1)
            slot_steps(act, step)

            def send(q, r):
                j = q * 2 + r
                act.wait_ge(both_added, j + 1)
                act.dma_start(dram(out_dram, j), some(x_all, j)).then_inc(out_sent[r], 16)
                act.wait_ge(out_sent[r], q * 16 + 16)
            with act.Fori(0, NB // 2) as q:
                for r in range(2):
                    send(q, r)

        @block.vector
        def _(dve):
            dve.wait_ge(const_in, 80)
            dve.tensor_tensor(a_sum[:], a_both[:, 0:1], a_both[:, 1:2], ALU.add).then_inc(a_summed, 1)

            def step(q, r, has):
                if has(0):
                    j, e, turn = batch(q, r, 0)
                    dve.wait_ge(ring_in[e], turn * 16 + 16)
                    dve.nop(nofuse=True)
                    for g in range(G):
                        last = dve.bn_stats(stats[:, g, :], x_ring[:, e, g, :])
                    last.then_inc(stat_step, 1)
                if has(5):
                    j5, e5, turn5 = batch(q, r, 5)
                    dve.wait_ge(logit_done, j5 + 1)
                    dve.tensor_tensor(some(logits, j5), bank[2][:, 0:G * E].rearrange("p (g e) -> p g e", g=G),
                                      b_gate[:].unsqueeze(1).to_broadcast([P, G, E]), ALU.add).then_inc(logit_copied, 1)
                if has(0):
                    dve.wait_ge(stat_step, 2 * j + 1)
                    dve.nop(nofuse=True)
                    for g in range(G):
                        last = dve.bn_aggr(mv[:, e, g, :], stats[:, g, :])
                    last.then_inc(stat_step, 1)
                if has(3):
                    j, e, turn = batch(q, r, 3)
                    dve.wait_ge(xe_step, 2 * j + 2)
                    dve.wait_ge(u_done, j + 1)
                    wait(dve, x2_kept[e], turn * 16)
                    dve.scalar_tensor_tensor(x2_ring[:, e].rearrange("p g d -> p (g d)"), bank[5 + e][:], 0.0,
                                             xe[:].rearrange("p g d -> p (g d)"), ALU.max, ALU.add).then_inc(x2_done, 1)
                if has(1):
                    j1, e1, turn1 = batch(q, r, 1)
                    dve.wait_ge(mask_made, j1 + 1)
                    dve.tensor_reduce(count[:, e1, :], mask[:, e1], AX.X, ALU.add).then_inc(counted, 1)
                if has(3):
                    dve.wait_ge(x2_done, j + 1)
                    dve.nop(nofuse=True)
                    for g in range(G):
                        last = dve.bn_stats(stats2[:, g, :], x2_ring[:, e, g, :])
                    last.then_inc(stat2_step, 1)
                    dve.wait_ge(stat2_step, 2 * j + 1)
                    dve.nop(nofuse=True)
                    for g in range(G):
                        last = dve.bn_aggr(mv2[:, g, :], stats2[:, g, :])
                    last.then_inc(stat2_step, 1)
                if has(1):
                    dve.wait_ge(h_done, j1 + 1)
                    dve.tensor_copy(score[:, e1, :], bank[0][:, 0:G]).then_inc(score_copied, 1)
                if has(2):
                    j, e, turn = batch(q, r, 2)
                    dve.wait_ge(soft_step, j * SOFT + SOFT)
                    wait(dve, aT_done, j)
                    for g in range(G):
                        last = dve.tensor_scalar(att[:, g, :], mask[:, e, g, :], att_a[:, e, g:g + 1], att_b[:, e, g:g + 1],
                                                 ALU.mult, ALU.add)
                    last.then_inc(att_done, 1)
                if has(0):
                    j, e, turn = batch(q, r, 0)
                    dve.wait_ge(rstd_step, 2 * j + 2)
                    wait(dve, xT_done, j - 1)
                    for g in range(G):
                        last = dve.tensor_scalar(xn[:, e, g, :], x_ring[:, e, g, :],
                                                 mv[:, e, g, 0:1], rstd[:, e, g:g + 1], ALU.subtract, ALU.mult)
                    last.then_inc(normed, 1)
                if has(3):
                    j, e, turn = batch(q, r, 3)
                    dve.wait_ge(rstd2_step, 2 * j + 2)
                    wait(dve, x2T_done, j - 1)
                    wait(dve, tok_out[e], turn * 16)
                    for g in range(G):
                        last = dve.tensor_scalar(xn2[:, e, g, :], x2_ring[:, e, g, :],
                                                 mv2[:, g, 0:1], rstd2[:, g:g + 1], ALU.subtract, ALU.mult)
                    last.then_inc(normed2, 1)

            attention_steps(dve, step)

            done = [0]

            def link(instruction):
                done[0] += 1
                instruction.then_inc(route, 1)
                dve.wait_ge(route, done[0])

            def over_experts(ap):
                return ap.unsqueeze(2).to_broadcast([P, B, E])

            rev_all = rev[:].unsqueeze(1).to_broadcast([P, B, E])
            dve.wait_ge(made_c, 1)
            dve.wait_ge(logit_copied, NB)
            source = logits[:]
            for k in range(K):
                link(dve.tensor_reduce(first[:, k, :], source, AX.X, ALU.max))
                link(dve.tensor_tensor(work[0], source, over_experts(first[:, k, :]), ALU.is_ge))
                link(dve.tensor_tensor(work[0], work[0], rev_all, ALU.mult))
                link(dve.tensor_reduce(key[:, k, :], work[0], AX.X, ALU.max))
                link(dve.tensor_tensor(chosen[:, k], over_experts(key[:, k, :]), rev_all, ALU.is_equal))
                if k == 0:
                    link(dve.scalar_tensor_tensor(work[1].rearrange("p b e -> p (b e)"), chosen[:, 0].rearrange("p b e -> p (b e)"),
                                                  LOW, logits[:].rearrange("p b e -> p (b e)"), ALU.mult, ALU.add))
                    source = work[1]
            dve.tensor_tensor(gap[:], first[:, 1, :], first[:, 0, :], ALU.subtract).then_inc(gap_made, 1)

            link(dve.tensor_tensor(member[:], chosen[:, 0].rearrange("p b e -> p e b"), chosen[:, 1].rearrange("p b e -> p e b"), ALU.add))
            dve.tensor_tensor_scan(upto[:].rearrange("p e b -> p (e b)"), reset[:].rearrange("p e b -> p (e b)"),
                                   member[:].rearrange("p e b -> p (e b)"), 0.0, ALU.mult, ALU.add).then_inc(totals, 1)
            dve.wait_ge(totals, 1)
            dve.wait_ge(counts, 1)
            link(dve.tensor_scalar(rows_i[:, 0, :], bank[7][:, 8:8 + E], float(P - 1), None, ALU.add))
            link(dve.tensor_scalar(rows_i[:, 1, :], rows_i[:, 0, :], 7, None, ALU.logical_shift_right))
            link(dve.tensor_copy(rows[:, 0, :], rows_i[:, 1, :]))
            link(dve.tensor_tensor_scan(rows[:, 1, :], ones[:, 0:E], rows[:, 0, :], 0.0, ALU.mult, ALU.add))
            link(dve.tensor_tensor(rows[:, 2, :], rows[:, 1, :], rows[:, 0, :], ALU.subtract))
            link(dve.scalar_tensor_tensor(rows[:, 3, :], rows[:, 2, :], float(P), bank[7][:, 0:E], ALU.mult, ALU.add))
            link(dve.tensor_tensor(upto[:], upto[:], member[:], ALU.subtract))
            link(dve.tensor_tensor(upto[:], upto[:], rows[:, 3, :].unsqueeze(2).to_broadcast([P, E, B]), ALU.add))
            for k in range(K):
                link(dve.tensor_tensor(work[0], chosen[:, k], upto[:].rearrange("p e b -> p b e"), ALU.mult))
                link(dve.tensor_reduce(pos[:, k * B:(k + 1) * B], work[0], AX.X, ALU.add))
            link(dve.tensor_copy(pos_i[:, 0, :], pos[:]))
            link(dve.tensor_scalar(pos_i[:, 1, :], pos_i[:, 0, :], P - 1, None, ALU.bitwise_and))
            link(dve.tensor_scalar(pos_i[:, 2, :], pos_i[:, 0, :], 7, None, ALU.logical_shift_right))
            link(dve.tensor_copy(pos_q[:], pos_i[:, 1, :]))
            dve.tensor_copy(pos_s[:], pos_i[:, 2, :]).then_inc(pos_made, 1)
            dve.wait_ge(pos_made, 1)

            def hot(q, r, first, last):
                n = q * RING + r
                wait(dve, hot_used, n - RING + 1)
                dve.tensor_scalar(hot_q[:, r, :], iota_q[:], pos_q[:, bass.ds(n, 1)], None, ALU.is_equal)
                dve.tensor_scalar(hot_s[:, r, 1, :], iota_s[:], pos_s[:, bass.ds(n, 1)], node[:], ALU.is_equal,
                                  ALU.mult).then_inc(hot_dve, 1)
            hot_steps(dve, hot)

            link(dve.tensor_tensor(past, iota_sf[:].unsqueeze(1).to_broadcast([1, E - 1, SLOTS]),
                                   rows[0:1, 1, 0:E - 1].unsqueeze(2).to_broadcast([1, E - 1, SLOTS]), ALU.is_ge))
            link(dve.tensor_reduce(slot_e[:], past.rearrange("p e s -> p s e"), AX.X, ALU.add))
            dve.tensor_copy(slot_expert[:], slot_e[:]).then_inc(experts_known, 1)

            dve.wait_ge(found_copied, 1)
            codes, nodes = found[:, 0, :], found[:, 1, :]
            link(dve.scalar_tensor_tensor(row[:, 0, :], codes, float(P), nodes, ALU.mult, ALU.add))
            link(dve.tensor_scalar(row[:, 1, :], codes, 0.0, None, ALU.is_equal))
            link(dve.tensor_tensor(row[:, 2, :], row[:, 1, :], pad_row[:], ALU.mult))
            link(dve.scalar_tensor_tensor(y_row[:], row[:, 0, :], float(-B * P), row[:, 2, :], ALU.add, ALU.add))
            link(dve.tensor_scalar(row[:, 3, :], codes, float(2 * B), float(-B * P), ALU.is_ge, ALU.mult))
            link(dve.tensor_tensor(row[:, 3, :], row[:, 3, :], row[:, 0, :], ALU.add))
            link(dve.tensor_scalar(gather_row[:], row[:, 3, :], float(-B * P), 0.0, ALU.add, ALU.max))

            dve.wait_ge(gap_exp, 1)
            link(dve.tensor_scalar(gate[:, 1, :], gap[:], 1.0, None, ALU.add))
            link(dve.reciprocal(gate[:, 0, :], gate[:, 1, :]))
            link(dve.tensor_tensor(gate[:, 1, :], gap[:], gate[:, 0, :], ALU.mult))

            def step(q, r, has):
                if has(0):
                    j, e, turn = slot(q, r, 0)
                    wait(dve, gathered[e], turn * 16)
                    dve.tensor_copy(gidx[e][:], gather_row[:, bass.ds(j, 1)]).then_inc(gidx_set, 1)
                if has(6):
                    j, e, turn = slot(q, r, 6)
                    wait(dve, scattered[e], turn * 16)
                    dve.tensor_copy(yidx[e][:], y_row[:, bass.ds(j, 1)]).then_inc(yidx_set, 1)
                if has(3):
                    j, e, turn = slot(q, r, 3)
                    dve.wait_ge(gT_high, j + 1)
                    dve.tensor_tensor(xg_lo[:, e % 2], bank[e % 2][:, 0:P], xg_hi[:, e % 2].bitcast(F32), ALU.subtract
                                      ).then_inc(gT_low, 1)
                if has(5):
                    j, e, turn = slot(q, r, 5)
                    dve.wait_ge(hT_high, j + 1)
                    dve.tensor_tensor(hT_lo[:, e % 2], bank[4 + e % 2][:], hT_hi[:, e % 2].bitcast(F32), ALU.subtract
                                      ).then_inc(hT_low_done, 1)
                if has(6):
                    j, e, turn = slot(q, r, 6)
                    dve.wait_ge(y_done, j + 1)
                    dve.tensor_reduce(y_sb[e], bank[6 + e % 2][:, 0:2 * D].rearrange("p (a d) -> p d a", a=2),
                                      AX.X, ALU.add).then_inc(y_copied, 1)
            slot_steps(dve, step)

            with dve.Fori(0, NB // 2) as q:
                for r in range(2):
                    j = q * 2 + r
                    for k, loaded, added in ((0, y0_in, first_added), (1, y1_in, both_added)):
                        dve.wait_ge(loaded[r], q * 16 + 16)
                        for g in range(G):
                            row_x = x_all[:, bass.ds(j * G + g, 1), :].rearrange("p o d -> p (o d)")
                            last = dve.scalar_tensor_tensor(row_x, y_in[k][:, r, g, :], gate[:, k, bass.ds(j * G + g, 1)], row_x,
                                                            ALU.mult, ALU.add)
                        last.then_inc(added, 1)
                        if k == 0:
                            dve.wait_ge(added, j + 1)

        @block.tensor
        def _(pe):
            pe.wait_ge(made_c, 1)
            pe.wait_ge(const_in, 80)
            pe.transpose(bank[0][:, 0:P], w_gat[:], ident[:]).then_inc(wT_done, 1)
            pe.wait_ge(wT_copied, 1)
            pe.wait_ge(a_summed, 1)
            pe.matmul(bank[1][:, 0:1], w_gatT[:], a_sum[:], start=True, stop=True).then_inc(ws_done, 1)
            pe.wait_ge(ws_copied, 1)

            def step(q, r, has):
                if has(1):
                    j, e, turn = batch(q, r, 1)
                    pe.wait_ge(normed, j + 1)
                    wait(pe, score_copied, j)
                    for g in range(G):
                        last = pe.transpose(bank[0][:, g * N:(g + 1) * N], xn[:, e, g, :], ident[:])
                    last.then_inc(xT_done, 1)
                if has(4):
                    j, e, turn = batch(q, r, 4)
                    pe.wait_ge(normed2, j + 1)
                    wait(pe, logit_copied, j)
                    for g in range(G):
                        last = pe.transpose(bank[2][:, g * N:(g + 1) * N], xn2[:, e, g, :], ident[:])
                    last.then_inc(x2T_done, 1)
                if has(1):
                    j, e, turn = batch(q, r, 1)
                    pe.wait_ge(xT_copied, j + 1)
                    wait(pe, h_copied, j - 1)
                    for g in range(G):
                        pe.matmul(bank[3 + e][:, g * D:(g + 1) * D], xnT[:, g, :], w_gat[:], start=True, stop=True)
                        last = pe.matmul(bank[0][:, g:g + 1], xnT[:, g, :], w_score[:], start=True, stop=True)
                    last.then_inc(h_done, 1)
                if has(4):
                    j, e, turn = batch(q, r, 4)
                    pe.wait_ge(x2T_copied, j + 1)
                    for g in range(G):
                        last = pe.matmul(bank[2][:, g * E:(g + 1) * E], xn2T[:, g, :], w_gate[:], start=True, stop=True)
                    last.then_inc(logit_done, 1)
                if has(2):
                    j, e, turn = batch(q, r, 2)
                    pe.wait_ge(att_done, j + 1)
                    wait(pe, aT_copied, j)
                    for g in range(G):
                        last = pe.transpose(bank[1][:, g * N:(g + 1) * N], att[:, g, :], ident[:])
                    last.then_inc(aT_done, 1)
                    pe.wait_ge(aT_copied, j + 1)
                    pe.wait_ge(h_copied, j + 1)
                    wait(pe, x2_done, j - 1)
                    for g in range(G):
                        last = pe.matmul(bank[5 + e][:, g * D:(g + 1) * D], attT[:, g, :], h_sb[:, e, g, :], start=True, stop=True)
                    last.then_inc(u_done, 1)

            attention_steps(pe, step)

            pe.wait_ge(totals, 1)
            pe.matmul(bank[7][:, 0:E], lower[:], upto[:, :, B - 1], start=True, stop=True)
            pe.matmul(bank[7][:, 8:8 + E], ones[:], upto[:, :, B - 1], start=True, stop=True).then_inc(counts, 1)

            def hot(q, r, first, last):
                n = q * RING + r
                pe.wait_ge(hot_dve, n + 1)
                pe.wait_ge(hot_pool, n + 1)
                pe.matmul(bank[0][:, 0:2 * SLOTS], hot_q[:, r, :], hot_s[:, r].rearrange("p a s -> p (a s)"),
                          start=first, stop=last).then_inc(hot_used, 1)
            hot_steps(pe, hot)

            pe.wait_ge(experts_known, 1)
            pe.wait_ge(w_low, NB)
            pe.wait_ge(b_joined, 16)
            pe.wait_ge(found_copied, 1)

            def step(q, r, has):
                if has(3):
                    j, e, turn = slot(q, r, 3)
                    pe.wait_ge(gathered[e], turn * 16 + 16)
                    wait(pe, gT_low, j - 1)
                    pe.transpose(bank[e % 2][:, 0:P], xg[e], ident[:]).then_inc(gT_done, 1)
                if has(4):
                    j, e, turn = slot(q, r, 4)
                    expert = pe.value_load(slot_expert[0:1, bass.ds(j, 1)], min_val=0, max_val=E - 1)
                    wait(pe, gelu_done, j - 1)
                    pre = bank[2 + e % 2][:]
                    pe.matmul(pre, ones_r[:], b1_hl[:, bass.ds(expert, 1), :], start=True, stop=False)
                    pe.wait_ge(gT_low, j + 1)
                    pe.matmul(pre, xg_hi[:, e % 2], w1_hi[:, bass.ds(expert, 1), :], start=False, stop=False)
                    pe.matmul(pre, xg_hi[:, e % 2], w1_lo[:, bass.ds(expert, 1), :], start=False, stop=False)
                    pe.matmul(pre, xg_lo[:, e % 2], w1_hi[:, bass.ds(expert, 1), :], start=False, stop=True).then_inc(pre_done, 1)
                if has(5):
                    j, e, turn = slot(q, r, 5)
                    pe.wait_ge(gelu_done, j + 1)
                    wait(pe, hT_low_done, j - 1)
                    for c in range(C):
                        last = pe.transpose(bank[4 + e % 2][:, c * P:(c + 1) * P], act_h[:, e % 2, c * P:(c + 1) * P], ident[:])
                    last.then_inc(hT_done, 1)
                if has(6):
                    j, e, turn = slot(q, r, 6)
                    expert = pe.value_load(slot_expert[0:1, bass.ds(j, 1)], min_val=0, max_val=E - 1)
                    wait(pe, y_copied, j - 1)
                    y = bank[6 + e % 2]
                    pe.wait_ge(hT_low_done, j + 1)
                    for c in range(C):
                        pe.matmul(y[:, 0:2 * D], hT_hi[:, e % 2, c * P:(c + 1) * P],
                                  w2_hl[:, bass.ds(expert, 1), c, :, :], start=(c == 0), stop=False)
                        pe.matmul(y[:, 0:D], hT_lo[:, e % 2, c * P:(c + 1) * P],
                                  w2_hl[:, bass.ds(expert, 1), c, 0, :], start=False, stop=False)
                    pe.matmul(y[:, 0:D], ones_r[:], b2_hl[:, bass.ds(expert, 1), :], start=False, stop=True).then_inc(y_done, 1)
            slot_steps(pe, step)


_INS = ['x', 'adj', 'L0_gnn_W', 'L0_gnn_a', 'L0_ffn_Wg', 'L0_ffn_bg', 'L0_ffn_W1', 'L0_ffn_b1', 'L0_ffn_W2', 'L0_ffn_b2']


def kernel(**inputs):
    import numpy as _np
    import concourse.bacc as _bacc
    from concourse import mybir as _mybir
    from concourse.bass_utils import run_bass_kernel_spmd as _run

    nc = _bacc.Bacc("TRN2", target_bir_lowering=False, num_devices=1)
    arrays, args = {}, []
    for name in _INS:
        a = _np.ascontiguousarray(inputs[name])
        arrays[f"in_{name}_dram"] = a
        args.append(nc.dram_tensor(f"in_{name}_dram", a.shape, _mybir.dt.from_np(a.dtype), kind="ExternalInput").ap())
    shape = inputs['x'].shape
    args.append(nc.dram_tensor("out_0_dram", shape, _mybir.dt.float32, kind="ExternalOutput").ap())
    gat_moe(nc, *args)
    r = _run(nc, [arrays], core_ids=[0])
    return r.results[0]["out_0_dram"]
```

```python
from contextlib import ExitStack

import concourse.bass as bass
from concourse import mybir

ALU = mybir.AluOpType
ACT = mybir.ActivationFunctionType
AX = mybir.AxisListType
F32 = mybir.dt.float32
F32R = mybir.dt.float32r
BF16 = mybir.dt.bfloat16
I32 = mybir.dt.int32

P = 128
ALPHA = 0.2
NEG = -9000000000000000.0
EPS = 1e-5
LOW = -3.0e38


def gat_moe(nc, x, adj, W, a, Wg, bg, W1, b1, W2, b2, out):
    B, N, D = x.shape
    E, _, H = W1.shape
    T = B * N
    G = 4
    NB = B // G
    C = H // P
    K = 2
    SLOTS = -(-(T * K // P + E - 1) // 4) * 4
    assert N == P and D == P and K * B == P and B % (2 * G) == 0 and SLOTS <= 256 and B * (K + 1) <= 256

    x_dram = x.rearrange("(b g) n d -> b n g d", g=G)
    adj_dram = adj.rearrange("(b g) n d -> b n g d", g=G)
    out_dram = out.rearrange("(b g) n d -> b n g d", g=G)

    with ExitStack() as ctx:
        def sb(name, shape, dt=F32):
            return ctx.enter_context(nc.sbuf_tensor(name, shape, dt))

        def sem(name):
            return ctx.enter_context(nc.semaphore(name))

        tok_dram = nc.dram_tensor("tok_dram", (T, D), F32, kind="Internal").ap()
        y_dram = nc.dram_tensor("y_dram", (K * T + SLOTS * P, D), F32, kind="Internal").ap()
        b_dram = nc.dram_tensor("b_dram", (2, E * (H + D)), F32R, kind="Internal").ap()
        tok_store = tok_dram.rearrange("(b g n) d -> b n g d", g=G, n=N)
        y_load = y_dram[0:K * T, :].rearrange("(k b g n) d -> k b n g d", k=K, g=G, n=N)

        bank = [ctx.enter_context(nc.psum_tensor(f"bank{i}", [P, 512], F32)) for i in range(8)]

        ident = sb("ident", [P, P])
        ones = sb("ones", [P, P])
        lower = sb("lower", [P, P])
        ones_r = sb("ones_r", [2, P], F32R)
        w_gat = sb("w_gat", [P, D])
        w_gatT = sb("w_gatT", [D, P])
        a_both = sb("a_both", [D, 2])
        a_sum = sb("a_sum", [D, 1])
        w_score = sb("w_score", [P, 1])
        w_gate = sb("w_gate", [P, E])
        b_gate = sb("b_gate", [P, E])
        HALF = H // 2
        w_raw = sb("w_raw", [P, 2, 2, HALF])
        w1_hi = sb("w1_hi", [P, E, H], F32R)
        w1_lo = sb("w1_lo", [P, E, H], F32R)
        w2_hl = sb("w2_hl", [P, E, C, 2, D], F32R)
        BR = E * (H + D) // P
        b_raw = sb("b_raw", [BR, P])
        b_high = sb("b_high", [BR, P], F32R)
        b_low = sb("b_low", [BR, P], F32R)
        b_hl = sb("b_hl", [2, E * (H + D)], F32R)
        b1_hl = b_hl[:, 0:E * H].rearrange("p (e h) -> p e h", e=E)
        b2_hl = b_hl[:, E * H:E * (H + D)].rearrange("p (e d) -> p e d", e=E)

        x_all = sb("x_all", [P, B, D])
        x_ring = sb("x_ring", [P, 2, G, D])
        x2_ring = sb("x2_ring", [P, 2, G, D])
        adj_ring = sb("adj_ring", [P, 2, G, N])
        mask = sb("mask", [P, 2, G, N])
        stats = sb("stats", [P, G, 6])
        mv = sb("mv", [P, 2, G, 2])
        rstd = sb("rstd", [P, 2, G])
        stats2 = sb("stats2", [P, G, 6])
        mv2 = sb("mv2", [P, 2, G, 2])
        rstd2 = sb("rstd2", [P, 2, G])
        back = sb("back", [P, 2, G])
        back2 = sb("back2", [P, 2, G])
        eps = sb("eps", [P, G])
        half = sb("half", [P, G])
        minus1 = sb("minus1", [P, G])
        xn = sb("xn", [P, 2, G, D])
        xnT = sb("xnT", [P, G, N])
        h_sb = sb("h_sb", [P, 2, G, D])
        edges = sb("edges", [P, 2, 2, G])
        alone = sb("alone", [P, 2, 2, G])
        leaky = sb("leaky", [P, 2, G])
        shift = sb("shift", [P, 2, G])
        expo = sb("expo", [P, 2, G])
        weigh = sb("weigh", [P, 5, G])
        att_a = sb("att_a", [P, G])
        att_b = sb("att_b", [P, G])
        act_h = sb("act_h", [P, 2, H])
        att = act_h[:, 0, :].rearrange("p (g n) -> p g n", g=G)
        attT = act_h[:, 1, :].rearrange("p (g n) -> p g n", g=G)
        exp_u = sb("exp_u", [P, G, D])
        xe = sb("xe", [P, G, D])
        x_less1 = sb("x_less1", [P, G, D])
        xn2 = sb("xn2", [P, 2, G, D])
        xn2T = sb("xn2T", [P, G, N])
        logits = sb("logits", [P, B, E])


        GROUPS = K * B
        rev = sb("rev", [P, E])
        iota_i = sb("iota_i", [P, P + SLOTS], I32)
        rev_i = sb("rev_i", [P, E], I32)
        node_i = sb("node_i", [P, 1], I32)
        slot_i = sb("slot_i", [P, SLOTS], I32)
        QUAD = 4
        iota_q = sb("iota_q", [P, P, QUAD], BF16)
        iota_s = sb("iota_s", [P, SLOTS, QUAD], BF16)
        iota_sf = sb("iota_sf", [1, SLOTS])
        code = sb("code", [P, GROUPS], BF16)
        node = sb("node", [P, 1])
        pad_row = sb("pad_row", [P, SLOTS])
        reset = sb("reset", [P, E, B])
        first = sb("first", [P, 2, B])
        work = [t[:].rearrange("p g n -> p (g n)").rearrange("p (b e) -> p b e", b=B) for t in (xnT, xn2T)]
        key = sb("key", [P, K, B])
        chosen = xn[:].rearrange("p k g d -> p (k g d)").rearrange("p (k b e) -> p k b e", k=K, b=B)
        member, upto = [adj_ring[:, i].rearrange("p g n -> p (g n)").rearrange("p (e b) -> p e b", e=E) for i in range(2)]
        rows = sb("rows", [P, 6, E])
        rows_i = sb("rows_i", [P, 2, E], I32)
        pos = sb("pos", [P, GROUPS])
        pos_i = sb("pos_i", [P, 3, GROUPS], I32)
        pos_q = sb("pos_q", [P, GROUPS], BF16)
        pos_s = sb("pos_s", [P, GROUPS], BF16)
        gap = sb("gap", [P, B])
        gate = sb("gate", [P, K, B])
        past = h_sb[0:1].rearrange("p k g d -> p (k g d)")[:, 0:(E - 1) * SLOTS].rearrange("p (e s) -> p e s", e=E - 1)
        slot_e = sb("slot_e", [1, SLOTS])
        slot_expert = sb("slot_expert", [1, SLOTS], I32)
        hot_q = sb("hot_q", [P, 2, P, QUAD], BF16)
        hot_s = sb("hot_s", [P, 2, SLOTS, QUAD], BF16)
        hot_sv = sb("hot_sv", [P, 2, 2, SLOTS, QUAD], BF16)
        places = w_raw[:].rearrange("p r k h -> p (r k h)")[:, 0:6 * SLOTS].rearrange("p (k s) -> p k s", k=6)
        found, row = places[:, 0:2, :], places[:, 2:6, :]
        gather_row = sb("gather_row", [P, SLOTS], I32)
        y_row = sb("y_row", [P, SLOTS], I32)

        gidx = [sb(f"gidx{i}", [P, 1], I32) for i in range(4)]
        yidx = [sb(f"yidx{i}", [P, 1], I32) for i in range(4)]
        xg = [x_less1[:, i, :] for i in range(4)]
        xg_hi = sb("xg_hi", [P, 2, P], F32R)
        xg_lo = sb("xg_lo", [P, 2, P], F32R)
        hT_hi = sb("hT_hi", [P, 2, H], F32R)
        hT_lo = sb("hT_lo", [P, 2, H], F32R)
        y_sb = [exp_u[:, i, :] for i in range(4)]
        y_in = [xn, h_sb]

        x_in = [sem(f"x_in{i}") for i in range(2)]
        ring_in = [sem(f"ring_in{i}") for i in range(2)]
        x2_kept = [sem(f"x2_kept{i}") for i in range(2)]
        adj_in = [sem(f"adj_in{i}") for i in range(2)]
        const_in, b_in = sem("const_in"), sem("b_in")
        w_in = [sem(f"w_in{i}") for i in range(4)]
        made, made_i, made_c = sem("made"), sem("made_i"), sem("made_c")
        a_summed, wT_done, wT_copied, ws_done, ws_copied = (
            sem("a_summed"), sem("wT_done"), sem("wT_copied"), sem("ws_done"), sem("ws_copied"))
        w_high, w_low = sem("w_high"), sem("w_low")
        b_parted = [sem(f"b_parted{i}") for i in range(2)]
        b_high_made, b_low_made, b_joined = sem("b_high_made"), sem("b_low_made"), sem("b_joined")
        stat_step, rstd_step, normed = sem("stat_step"), sem("rstd_step"), sem("normed")
        xT_done, xT_copied = sem("xT_done"), sem("xT_copied")
        h_done, h_copied = sem("h_done"), sem("h_copied")
        mask_made, counted = sem("mask_made"), sem("counted")
        soft_step, soft_exp, att_done = sem("soft_step"), sem("soft_exp"), sem("att_done")
        aT_done, aT_copied = sem("aT_done"), sem("aT_copied")
        u_done, u_exp, x2_done = sem("u_done"), sem("u_exp"), sem("x2_done")
        stat2_step, rstd2_step, normed2 = sem("stat2_step"), sem("rstd2_step"), sem("normed2")
        x2T_done, x2T_copied = sem("x2T_done"), sem("x2T_copied")
        logit_done, logit_copied = sem("logit_done"), sem("logit_copied")
        tok_out = [sem(f"tok_out{i}") for i in range(2)]
        tokens_stored = sem("tokens_stored")
        route = sem("route")
        totals, counts = sem("totals"), sem("counts")
        gap_made, gap_exp, gate_step = sem("gap_made"), sem("gap_exp"), sem("gate_step")
        pos_made = sem("pos_made")
        hot_coded, hot_used = sem("hot_coded"), sem("hot_used")
        hot_made, hot_scaled = sem("hot_made"), sem("hot_scaled")
        back_made, back2_made = sem("back_made"), sem("back2_made")
        elu_made, less1_made = sem("elu_made"), sem("less1_made")
        found_copied = sem("found_copied")
        experts_known = sem("experts_known")
        gidx_set, yidx_set = sem("gidx_set"), sem("yidx_set")
        gathered = [sem(f"gathered{i}") for i in range(4)]
        scattered = [sem(f"scattered{i}") for i in range(4)]
        gT_done, gT_high, gT_low = sem("gT_done"), sem("gT_high"), sem("gT_low")
        pre_done, gelu_done = sem("pre_done"), sem("gelu_done")
        hT_done, hT_high, hT_low_done = sem("hT_done"), sem("hT_high"), sem("hT_low_done")
        y_done, y_copied = sem("y_done"), sem("y_copied")
        y0_in = [sem(f"y0_in{i}") for i in range(2)]
        y1_in = [sem(f"y1_in{i}") for i in range(2)]
        first_added, both_added = sem("first_added"), sem("both_added")
        out_sent = [sem(f"out_sent{i}") for i in range(2)]

        HEAD, SOFT = 4, 11

        def attention_steps(eng, step):
            def at(i):
                step(i // 2, i % 2, lambda k: 0 <= i - k < NB)
            for i in range(6):
                at(i)
            with eng.Fori(3, NB // 2) as q:
                for r in range(2):
                    step(q, r, lambda k: True)
            for i in range(NB, NB + 6):
                at(i)

        def batch(q, r, k):
            e = (r - k) % 2
            turn = q + (r - k - e) // 2
            return turn * 2 + e, e, turn

        def slot_steps(eng, step):
            def at(i):
                step(i // 4, i % 4, lambda k: 0 <= i - k < SLOTS)
            for i in range(8):
                at(i)
            with eng.Fori(2, SLOTS // 4) as q:
                for r in range(4):
                    step(q, r, lambda k: True)
            for i in range(SLOTS, SLOTS + 7):
                at(i)

        def slot(q, r, k):
            e = (r - k) % 4
            turn = q + (r - k - e) // 4
            return turn * 4 + e, e, turn

        def hot_steps(eng, step):
            step(0, 0, True, False)
            step(1, 1, False, False)
            with eng.Fori(1, GROUPS // QUAD // 2 - 1) as q:
                for r in range(2):
                    step(q * 2 + r, r, False, False)
            step(GROUPS // QUAD - 2, 0, False, False)
            step(GROUPS // QUAD - 1, 1, False, True)

        def wait(eng, semaphore, value):
            if not isinstance(value, int) or value > 0:
                eng.wait_ge(semaphore, value)

        def expert_of(t, e):
            return t[bass.ds(e, 1)].rearrange("o a b -> (o a) b")

        def one(t, e):
            v = t[:, bass.ds(e, 1)]
            return v.rearrange("p o h -> p (o h)") if len(v.shape) == 3 else v.rearrange("p o c k d -> p (o c) k d")

        def flat(ap):
            return ap.rearrange("p g d -> p (g d)")

        def some(t, j):
            return t[:, bass.ds(j * G, G), :]

        def dram(t, j):
            return t[bass.ds(j, 1)].rearrange("o n g d -> (o n) g d")

        block = ctx.enter_context(nc.Block())

        @block.sync
        def _(sp):
            def load(q, r, has):
                if has(0):
                    j, e, turn = batch(q, r, 0)
                    wait(sp, normed, j - 1)
                    sp.dma_start(x_ring[:, e], dram(x_dram, j)).then_inc(ring_in[e], 16)
                    wait(sp, x_in[e], turn * 16)
                    sp.dma_start(some(x_all, j), dram(x_dram, j)).then_inc(x_in[e], 16)
                    wait(sp, mask_made, j - 1)
                    sp.dma_start(adj_ring[:, e], dram(adj_dram, j)).then_inc(adj_in[e], 16)
                if has(0):
                    wait(sp, w_low, j - 1)
                    sp.dma_start(w_raw[:, e, 0, :], expert_of(W1, turn)[:, e * HALF:(e + 1) * HALF]
                                 ).then_inc(w_in[e], 16)
                    sp.dma_start(w_raw[:, e, 1, :].rearrange("p (c d) -> p c d", d=D),
                                 expert_of(W2, turn).rearrange("(c p) d -> p c d", p=P)[:, e * C // 2:(e + 1) * C // 2, :]
                                 ).then_inc(w_in[2 + e], 16)
                if has(4):
                    j, e, turn = batch(q, r, 4)
                    sp.wait_ge(normed2, j + 1)
                    sp.dma_start(dram(tok_store, j), xn2[:, e]).then_inc(tok_out[e], 16)
                    sp.dma_start(some(x_all, j), x2_ring[:, e]).then_inc(x2_kept[e], 16)

            sp.dma_start(w_gat[:], W).then_inc(const_in, 16)
            for t in range(2):
                sp.dma_start(a_both[:, t:t + 1], a[t * D:(t + 1) * D, :]).then_inc(const_in, 16)
            sp.dma_start(w_gate[:], Wg).then_inc(const_in, 16)
            sp.dma_start(b_gate[:], bg.partition_broadcast(P)).then_inc(const_in, 16)
            attention_steps(sp, load)

            for e in range(2):
                sp.wait_ge(tok_out[e], 16 * NB // 2)
            sp.sem_inc(tokens_stored, 1)

            for e in range(4):
                sp.wait_ge(scattered[e], 16 * SLOTS // 4)
            def fetch(q, r):
                j = q * 2 + r
                wait(sp, both_added, j - 1)
                sp.dma_start(y_in[0][:, r], y_load[0, bass.ds(j, 1)].rearrange("o n g d -> (o n) g d")).then_inc(y0_in[r], 16)
                sp.dma_start(y_in[1][:, r], y_load[1, bass.ds(j, 1)].rearrange("o n g d -> (o n) g d")).then_inc(y1_in[r], 16)
            for r in range(2):
                fetch(0, r)
            with sp.Fori(1, NB // 2) as q:
                for r in range(2):
                    fetch(q, r)

        @block.gpsimd
        def _(pool):
            pool.memset(ident[:], 0.0)
            pool.memset(ones[:], 1.0)
            pool.memset(lower[:], 1.0)
            pool.memset(half[:], -0.5)
            pool.memset(minus1[:], -1.0)
            pool.memset(eps[:], EPS)
            pool.iota(iota_q[:], pattern=[[1, P], [0, QUAD]], base=0, channel_multiplier=0,
                      allow_small_or_imprecise_dtypes=True)
            pool.iota(iota_s[:], pattern=[[1, SLOTS], [0, QUAD]], base=0, channel_multiplier=0,
                      allow_small_or_imprecise_dtypes=True)
            pool.memset(ones_r[:].bitcast(F32), 1.0)
            pool.memset(reset[:], 1.0)
            pool.iota(iota_i[:, 0:SLOTS], pattern=[[P, SLOTS]], base=K * T + B * P, channel_multiplier=1)
            pool.iota(iota_i[:, SLOTS:SLOTS + P], pattern=[[1, P]], base=B, channel_multiplier=0).then_inc(made_i, 1)
            pool.wait_ge(made_i, 1)
            pool.affine_select(out=ident[:], in_=ident[:], compare_op=ALU.not_equal, fill=1.0, base=0,
                               pattern=[[-1, P]], channel_multiplier=1)
            pool.affine_select(out=lower[:], in_=lower[:], compare_op=ALU.is_ge, fill=0.0, base=-1,
                               pattern=[[1, P]], channel_multiplier=-1)
            pool.memset(reset[:, :, 0:1], 0.0)
            pool.iota(rev_i[:], pattern=[[-1, E]], base=E, channel_multiplier=0)
            pool.iota(node_i[:], pattern=[[1, 1]], base=0, channel_multiplier=1)
            pool.iota(slot_i[:], pattern=[[1, SLOTS]], base=0, channel_multiplier=0).then_inc(made, 1)
            pool.wait_ge(made, 1)
            for dst, src in ((iota_sf[:], slot_i[0:1, :]),
                             (pad_row[:], iota_i[:, 0:SLOTS]), (code[:], iota_i[:, SLOTS:SLOTS + P]),
                             (rev[:], rev_i[:]), (node[:], node_i[:])):
                last = pool.tensor_copy(dst, src)
            last.then_inc(made_c, 1)

            def step(q, r, has):
                if has(0):
                    j, e, turn = batch(q, r, 0)
                    wait(pool, normed, j - 1)
                    pool.wait_ge(stat_step, 2 * j + 2)
                    pool.nop(nofuse=True)
                    pool.tensor_tensor(mv[:, e, :, 1], mv[:, e, :, 1], eps[:], ALU.add).then_inc(rstd_step, 1)
                    pool.wait_ge(rstd_step, 2 * j + 1)
                    pool.tensor_tensor(rstd[:, e, :], mv[:, e, :, 1], half[:], ALU.pow).then_inc(rstd_step, 1)
                if has(2):
                    j, e, turn = batch(q, r, 2)
                    pool.wait_ge(x_in[e], turn * 16 + 16)
                    wait(pool, elu_made, j)
                    pool.tensor_tensor(x_less1[:], some(x_all, j), minus1[:, 0:1].unsqueeze(2).to_broadcast([P, G, D]),
                                       ALU.add).then_inc(less1_made, 1)
                if has(3):
                    j, e, turn = batch(q, r, 3)
                    wait(pool, normed2, j - 1)
                    pool.wait_ge(stat2_step, 2 * j + 2)
                    pool.tensor_tensor(mv2[:, e, :, 1], mv2[:, e, :, 1], eps[:], ALU.add).then_inc(rstd2_step, 1)
                    pool.wait_ge(rstd2_step, 2 * j + 1)
                    pool.tensor_tensor(rstd2[:, e, :], mv2[:, e, :, 1], half[:], ALU.pow).then_inc(rstd2_step, 1)
                if has(1):
                    j, e, turn = batch(q, r, 1)
                    pool.wait_ge(w_high, j + 1)
                    w1_part = slice(e * HALF, (e + 1) * HALF)
                    w2_part = slice(e * C // 2, (e + 1) * C // 2)
                    pool.tensor_tensor(one(w1_lo, turn)[:, w1_part], w_raw[:, e, 0, :],
                                       one(w1_hi, turn)[:, w1_part].bitcast(F32), ALU.subtract)
                    pool.tensor_tensor(one(w2_hl, turn)[:, w2_part, 1, :], w_raw[:, e, 1, :].rearrange("p (c d) -> p c d", d=D),
                                       one(w2_hl, turn)[:, w2_part, 0, :].bitcast(F32), ALU.subtract).then_inc(w_low, 1)

            attention_steps(pool, step)

            pool.wait_ge(b_high_made, 1)
            pool.tensor_tensor(b_low[:], b_raw[:], b_high[:].bitcast(F32), ALU.subtract).then_inc(b_low_made, 1)
            pool.wait_ge(b_low_made, 1)
            pool.dma_start(b_dram[0].rearrange("(r p) -> r p", p=P), b_high[:]).then_inc(b_parted[0], 16)
            pool.dma_start(b_dram[1].rearrange("(r p) -> r p", p=P), b_low[:]).then_inc(b_parted[1], 16)
            pool.wait_ge(b_parted[0], 16)
            pool.wait_ge(b_parted[1], 16)
            pool.dma_start(b_hl[:], b_dram).then_inc(b_joined, 16)

            def step(q, r, has):
                if has(0):
                    j, e, turn = slot(q, r, 0)
                    pool.wait_ge(gidx_set, j + 1)
                    wait(pool, gT_done, j - 3)
                    pool.nop(nofuse=True)
                    pool.indirect_dma_start(xg[e], None, tok_dram, bass.IndirectOffsetOnAxis(ap=gidx[e][:], axis=0)
                                            ).then_inc(gathered[e], 16)
                if has(6):
                    j, e, turn = slot(q, r, 6)
                    pool.wait_ge(yidx_set, j + 1)
                    pool.wait_ge(y_copied, j + 1)
                    pool.nop(nofuse=True)
                    pool.indirect_dma_start(y_dram, bass.IndirectOffsetOnAxis(ap=yidx[e][:], axis=0), y_sb[e], None
                                            ).then_inc(scattered[e], 16)
            pool.wait_ge(tokens_stored, 1)
            slot_steps(pool, step)

        @block.scalar
        def _(act):
            b1_rows = b1.rearrange("e (c p) -> (e c) p", p=P)
            act.dma_start(b_raw[0:E * C, :], b1_rows).then_inc(b_in, 16)
            act.dma_start(b_raw[E * C:BR, :], b2).then_inc(b_in, 16)
            act.wait_ge(wT_done, 1)
            act.activation(w_gatT[:], bank[0][:, 0:P], ACT.Copy).then_inc(wT_copied, 1)
            act.wait_ge(ws_done, 1)
            act.activation(w_score[:], bank[1][:, 0:1], ACT.Copy).then_inc(ws_copied, 1)

            def step(q, r, has):
                if has(2):
                    j, e, turn = batch(q, r, 2)
                    act.wait_ge(soft_step, j * SOFT + HEAD)
                    act.activation(expo[:, 0, :], shift[:, 0, :], ACT.Exp)
                    act.activation(expo[:, 1, :], shift[:, 1, :], ACT.Exp, scale=-1.0).then_inc(soft_exp, 1)
                if has(1):
                    j, e, turn = batch(q, r, 1)
                    act.wait_ge(back_made, j + 1)
                    wait(act, xT_done, j - 1)
                    for g in range(G):
                        last = act.activation(xn[:, e, g, :], x_ring[:, e, g, :], ACT.Identity,
                                              bias=back[:, e, g:g + 1], scale=rstd[:, e, g:g + 1])
                    last.then_inc(normed, 1)
                if has(4):
                    j, e, turn = batch(q, r, 4)
                    act.wait_ge(back2_made, j + 1)
                    wait(act, x2T_done, j - 1)
                    wait(act, tok_out[e], turn * 16)
                    for g in range(G):
                        last = act.activation(xn2[:, e, g, :], x2_ring[:, e, g, :], ACT.Identity,
                                              bias=back2[:, e, g:g + 1], scale=rstd2[:, e, g:g + 1])
                    last.then_inc(normed2, 1)
                if has(1):
                    j, e, turn = batch(q, r, 1)
                    act.wait_ge(xT_done, j + 1)
                    wait(act, h_done, j)
                    act.activation(xnT[:].rearrange("p g n -> p (g n)"), bank[0][:], ACT.Copy).then_inc(xT_copied, 1)
                if has(4):
                    j, e, turn = batch(q, r, 4)
                    act.wait_ge(x2T_done, j + 1)
                    wait(act, logit_done, j)
                    act.activation(xn2T[:].rearrange("p g n -> p (g n)"), bank[2][:], ACT.Copy).then_inc(x2T_copied, 1)
                if has(2):
                    j, e, turn = batch(q, r, 2)
                    act.wait_ge(aT_done, j + 1)
                    wait(act, u_done, j)
                    act.activation(attT.rearrange("p g n -> p (g n)"), bank[1][:], ACT.Copy).then_inc(aT_copied, 1)
                if has(1):
                    j, e, turn = batch(q, r, 1)
                    act.wait_ge(h_done, j + 1)
                    wait(act, u_done, j - 1)
                    act.activation(h_sb[:, e].rearrange("p g d -> p (g d)"), bank[3 + e][:], ACT.Copy).then_inc(h_copied, 1)
                if has(0):
                    j, e, turn = batch(q, r, 0)
                    act.wait_ge(w_in[e], turn * 16 + 16)
                    act.activation(one(w1_hi, turn)[:, e * HALF:(e + 1) * HALF], w_raw[:, e, 0, :], ACT.Copy)
                    act.wait_ge(w_in[2 + e], turn * 16 + 16)
                    act.activation(one(w2_hl, turn)[:, e * C // 2:(e + 1) * C // 2, 0, :],
                                   w_raw[:, e, 1, :].rearrange("p (c d) -> p c d", d=D), ACT.Copy).then_inc(w_high, 1)
                if has(2):
                    j, e, turn = batch(q, r, 2)
                    act.wait_ge(u_done, j + 1)
                    wait(act, elu_made, j)
                    act.activation(exp_u[:].rearrange("p g d -> p (g d)"), bank[5 + e][:], ACT.Exp).then_inc(u_exp, 1)

            attention_steps(act, step)

            act.wait_ge(b_in, 32)
            act.activation(b_high[:], b_raw[:], ACT.Copy).then_inc(b_high_made, 1)

            act.wait_ge(gap_made, 1)
            act.activation(gap[:], gap[:], ACT.Exp).then_inc(gap_exp, 1)

            def hot(n, r, first, last):
                act.wait_ge(hot_made, n + 1)
                wait(act, hot_used, n - 1)
                act.activation(hot_sv[:, r, 1].rearrange("p s g -> p (s g)"), hot_s[:, r].rearrange("p s g -> p (s g)"),
                               ACT.Copy, scale=node[:]).then_inc(hot_scaled, 1)
            hot_steps(act, hot)
            act.wait_ge(hot_used, GROUPS // QUAD)
            act.wait_ge(w_low, NB)
            act.activation(found.rearrange("p a s -> p (a s)"), bank[0][:, 0:2 * SLOTS], ACT.Copy).then_inc(found_copied, 1)

            def step(q, r, has):
                if has(3):
                    j, e, turn = slot(q, r, 3)
                    act.wait_ge(gT_done, j + 1)
                    wait(act, pre_done, j - 1)
                    act.activation(xg_hi[:, e % 2], bank[e % 2][:, 0:P], ACT.Copy).then_inc(gT_high, 1)
                if has(4):
                    j, e, turn = slot(q, r, 4)
                    act.wait_ge(pre_done, j + 1)
                    wait(act, hT_done, j - 1)
                    act.activation(act_h[:, e % 2], bank[2 + e % 2][:], ACT.Gelu).then_inc(gelu_done, 1)
                if has(5):
                    j, e, turn = slot(q, r, 5)
                    act.wait_ge(hT_done, j + 1)
                    wait(act, y_done, j - 1)
                    act.activation(hT_hi[:, e % 2], bank[4 + e % 2][:], ACT.Copy).then_inc(hT_high, 1)
            slot_steps(act, step)

            def send(q, r):
                j = q * 2 + r
                act.wait_ge(both_added, j + 1)
                wait(act, out_sent[r], q * 16)
                act.dma_start(dram(out_dram, j), some(x_all, j)).then_inc(out_sent[r], 16)
            for r in range(2):
                send(0, r)
            with act.Fori(1, NB // 2) as q:
                for r in range(2):
                    send(q, r)
            for r in range(2):
                act.wait_ge(out_sent[r], 16 * NB // 2)

        @block.vector
        def _(dve):
            dve.wait_ge(const_in, 80)
            dve.tensor_tensor(a_sum[:], a_both[:, 0:1], a_both[:, 1:2], ALU.add).then_inc(a_summed, 1)

            def step(q, r, has):
                if has(0):
                    j0, e0, turn0 = batch(q, r, 0)
                    dve.wait_ge(ring_in[e0], turn0 * 16 + 16)
                    dve.nop(nofuse=True)
                tail = []
                if has(2):
                    j2, e2, turn2 = batch(q, r, 2)
                    w = [weigh[:, k, :] for k in range(5)]
                    tail = [
                        lambda: dve.tensor_tensor(expo[:], expo[:], alone[:, e2], ALU.max),
                        lambda: dve.tensor_tensor(weigh[:, 0:2, :], expo[:], edges[:, e2], ALU.mult),
                        lambda: dve.tensor_tensor(w[2], w[0], w[1], ALU.add),
                        lambda: dve.reciprocal(w[3], w[2]),
                        lambda: dve.tensor_tensor(w[4], expo[:, 0, :], expo[:, 1, :], ALU.subtract),
                        lambda: dve.tensor_tensor(att_b[:], expo[:, 1, :], w[3], ALU.mult),
                        lambda: dve.tensor_tensor(att_a[:], w[4], w[3], ALU.mult),
                    ]
                for g in range(max(G, len(tail))):
                    if has(0) and g < G:
                        last = dve.bn_stats(stats[:, g, :], x_ring[:, e0, g, :])
                        if g == G - 1:
                            last.then_inc(stat_step, 1)
                    if g < len(tail):
                        if g == 0:
                            dve.wait_ge(soft_exp, j2 + 1)
                        elif g != 4:
                            dve.wait_ge(soft_step, j2 * SOFT + HEAD + g)
                        tail[g]().then_inc(soft_step, 1)
                if has(0):
                    dve.wait_ge(stat_step, 2 * j0 + 1)
                    dve.nop(nofuse=True)
                    for g in range(G):
                        last = dve.bn_aggr(mv[:, e0, g, :], stats[:, g, :])
                    last.then_inc(stat_step, 1)
                if has(2):
                    dve.wait_ge(soft_step, j2 * SOFT + SOFT)
                    wait(dve, aT_done, j2)
                    for g in range(G):
                        last = dve.tensor_scalar(att[:, g, :], mask[:, e2, g, :], att_a[:, g:g + 1], att_b[:, g:g + 1],
                                                 ALU.mult, ALU.add)
                    last.then_inc(att_done, 1)
                if has(3):
                    j3, e3, turn3 = batch(q, r, 3)
                    dve.wait_ge(u_exp, j3 + 1)
                    dve.wait_ge(less1_made, j3 + 1)
                    dve.scalar_tensor_tensor(flat(xe[:]), flat(exp_u[:]), 1.0, flat(x_less1[:]), ALU.min, ALU.add
                                             ).then_inc(elu_made, 1)
                if has(0):
                    dve.wait_ge(adj_in[e0], turn0 * 16 + 16)
                    wait(dve, att_done, j0 - 1)
                    dve.tensor_scalar(mask[:, e0], adj_ring[:, e0], 0.0, None, ALU.is_gt).then_inc(mask_made, 1)
                if has(3):
                    dve.wait_ge(elu_made, j3 + 1)
                    wait(dve, x2_kept[e3], turn3 * 16)
                    wait(dve, normed2, j3 - 1)
                    dve.scalar_tensor_tensor(flat(x2_ring[:, e3]), bank[5 + e3][:], 0.0, flat(xe[:]), ALU.max, ALU.add
                                             ).then_inc(x2_done, 1)
                if has(0):
                    dve.wait_ge(mask_made, j0 + 1)
                    dve.tensor_reduce(edges[:, e0, 0, :], mask[:, e0], AX.X, ALU.add).then_inc(counted, 1)
                if has(5):
                    j5, e5, turn5 = batch(q, r, 5)
                    dve.wait_ge(logit_done, j5 + 1)
                    dve.tensor_tensor(some(logits, j5), bank[2][:, 0:G * E].rearrange("p (g e) -> p g e", g=G),
                                      b_gate[:].unsqueeze(1).to_broadcast([P, G, E]), ALU.add).then_inc(logit_copied, 1)
                if has(3):
                    dve.wait_ge(x2_done, j3 + 1)
                    dve.nop(nofuse=True)
                    for g in range(G):
                        last = dve.bn_stats(stats2[:, g, :], x2_ring[:, e3, g, :])
                    last.then_inc(stat2_step, 1)
                head = []
                if has(1):
                    j1, e1, turn1 = batch(q, r, 1)
                    head = [
                        lambda: dve.tensor_copy(leaky[:, 0, :], bank[0][:, 0:G]),
                        lambda: dve.scalar_tensor_tensor(leaky[:, 1, :], leaky[:, 0, :], ALPHA, leaky[:, 0, :], ALU.mult, ALU.max),
                        lambda: dve.tensor_scalar(shift[:, 0, :], leaky[:, 1, :], -NEG, 0.0, ALU.add, ALU.min),
                        lambda: dve.tensor_scalar(shift[:, 1, :], leaky[:, 1, :], -NEG, 0.0, ALU.add, ALU.max),
                    ]
                flags = []
                if has(0):
                    flags = [
                        lambda: dve.tensor_scalar(edges[:, e0, 1, :], edges[:, e0, 0, :], -1.0, float(N), ALU.mult, ALU.add),
                        lambda: dve.tensor_scalar(alone[:, e0, 0, :], edges[:, e0, 0, :], float(N), None, ALU.is_ge),
                        lambda: dve.tensor_scalar(alone[:, e0, 1, :], edges[:, e0, 0, :], 0.0, None, ALU.is_equal),
                    ]
                    dve.wait_ge(counted, j0 + 1)
                for n in range(4):
                    if head:
                        dve.wait_ge(*((h_done, j1 + 1) if n == 0 else (soft_step, j1 * SOFT + min(n, 2))))
                        head[n]().then_inc(soft_step, 1)
                    if n < len(flags):
                        flags[n]()
                if has(3):
                    dve.wait_ge(stat2_step, 2 * j3 + 1)
                    dve.nop(nofuse=True)
                    for g in range(G):
                        last = dve.bn_aggr(mv2[:, e3, g, :], stats2[:, g, :])
                    last.then_inc(stat2_step, 1)
                if has(0):
                    dve.wait_ge(rstd_step, 2 * j0 + 2)
                    dve.scalar_tensor_tensor(back[:, e0, :], mv[:, e0, :, 0], -1.0, rstd[:, e0, :], ALU.mult, ALU.mult
                                             ).then_inc(back_made, 1)
                if has(3):
                    dve.wait_ge(rstd2_step, 2 * j3 + 2)
                    dve.scalar_tensor_tensor(back2[:, e3, :], mv2[:, e3, :, 0], -1.0, rstd2[:, e3, :], ALU.mult, ALU.mult
                                             ).then_inc(back2_made, 1)

            attention_steps(dve, step)

            done = [0]

            def link(instruction):
                done[0] += 1
                instruction.then_inc(route, 1)
                dve.wait_ge(route, done[0])

            def over_experts(ap):
                return ap.unsqueeze(2).to_broadcast([P, B, E])

            rev_all = rev[:].unsqueeze(1).to_broadcast([P, B, E])
            dve.wait_ge(made_c, 1)
            dve.wait_ge(logit_copied, NB)
            source = logits[:]
            for k in range(K):
                link(dve.tensor_reduce(first[:, k, :], source, AX.X, ALU.max))
                link(dve.tensor_tensor(work[0], source, over_experts(first[:, k, :]), ALU.is_ge))
                link(dve.tensor_tensor(work[0], work[0], rev_all, ALU.mult))
                link(dve.tensor_reduce(key[:, k, :], work[0], AX.X, ALU.max))
                link(dve.tensor_tensor(chosen[:, k], over_experts(key[:, k, :]), rev_all, ALU.is_equal))
                if k == 0:
                    link(dve.scalar_tensor_tensor(work[1].rearrange("p b e -> p (b e)"), chosen[:, 0].rearrange("p b e -> p (b e)"),
                                                  LOW, logits[:].rearrange("p b e -> p (b e)"), ALU.mult, ALU.add))
                    source = work[1]
            dve.tensor_tensor(gap[:], first[:, 1, :], first[:, 0, :], ALU.subtract).then_inc(gap_made, 1)

            link(dve.tensor_tensor(member, chosen[:, 0].rearrange("p b e -> p e b"), chosen[:, 1].rearrange("p b e -> p e b"), ALU.add))
            dve.tensor_tensor_scan(upto.rearrange("p e b -> p (e b)"), reset[:].rearrange("p e b -> p (e b)"),
                                   member.rearrange("p e b -> p (e b)"), 0.0, ALU.mult, ALU.add).then_inc(totals, 1)
            dve.wait_ge(totals, 1)
            dve.wait_ge(counts, 1)
            link(dve.tensor_scalar(rows_i[:, 0, :], bank[7][:, 8:8 + E], float(P - 1), None, ALU.add))
            link(dve.tensor_scalar(rows_i[:, 1, :], rows_i[:, 0, :], 7, None, ALU.logical_shift_right))
            link(dve.tensor_copy(rows[:, 0, :], rows_i[:, 1, :]))
            link(dve.tensor_tensor_scan(rows[:, 1, :], ones[:, 0:E], rows[:, 0, :], 0.0, ALU.mult, ALU.add))
            link(dve.tensor_tensor(rows[:, 2, :], rows[:, 1, :], rows[:, 0, :], ALU.subtract))
            link(dve.scalar_tensor_tensor(rows[:, 3, :], rows[:, 2, :], float(P), bank[7][:, 0:E], ALU.mult, ALU.add))
            link(dve.tensor_tensor(upto, upto, member, ALU.subtract))
            link(dve.tensor_tensor(upto, upto, rows[:, 3, :].unsqueeze(2).to_broadcast([P, E, B]), ALU.add))
            for k in range(K):
                link(dve.tensor_tensor(work[0], chosen[:, k], upto.rearrange("p e b -> p b e"), ALU.mult))
                link(dve.tensor_reduce(pos[:, k * B:(k + 1) * B], work[0], AX.X, ALU.add))
            link(dve.tensor_copy(pos_i[:, 0, :], pos[:]))
            link(dve.tensor_scalar(pos_i[:, 1, :], pos_i[:, 0, :], P - 1, None, ALU.bitwise_and))
            link(dve.tensor_scalar(pos_i[:, 2, :], pos_i[:, 0, :], 7, None, ALU.logical_shift_right))
            link(dve.tensor_copy(pos_q[:], pos_i[:, 1, :]))
            dve.tensor_copy(pos_s[:], pos_i[:, 2, :]).then_inc(pos_made, 1)
            dve.wait_ge(pos_made, 1)

            def hot(n, r, first, last):
                def per(t, width):
                    return t[:, bass.ds(n * QUAD, QUAD)].unsqueeze(1).to_broadcast([P, width, QUAD])
                wait(dve, hot_used, n - 1)
                wait(dve, hot_scaled, n - 1)
                dve.tensor_tensor(hot_s[:, r], iota_s[:], per(pos_s, SLOTS), ALU.is_equal).then_inc(hot_made, 1)
                dve.tensor_tensor(hot_q[:, r], iota_q[:], per(pos_q, P), ALU.is_equal)
                dve.wait_ge(hot_made, n + 1)
                dve.tensor_tensor(hot_sv[:, r, 0], hot_s[:, r], per(code, SLOTS), ALU.mult).then_inc(hot_coded, 1)
            hot_steps(dve, hot)

            link(dve.tensor_tensor(past, iota_sf[:].unsqueeze(1).to_broadcast([1, E - 1, SLOTS]),
                                   rows[0:1, 1, 0:E - 1].unsqueeze(2).to_broadcast([1, E - 1, SLOTS]), ALU.is_ge))
            link(dve.tensor_reduce(slot_e[:], past.rearrange("p e s -> p s e"), AX.X, ALU.add))
            dve.tensor_copy(slot_expert[:], slot_e[:]).then_inc(experts_known, 1)

            dve.wait_ge(found_copied, 1)
            codes, nodes = found[:, 0, :], found[:, 1, :]
            link(dve.scalar_tensor_tensor(row[:, 0, :], codes, float(P), nodes, ALU.mult, ALU.add))
            link(dve.tensor_scalar(row[:, 1, :], codes, 0.0, None, ALU.is_equal))
            link(dve.tensor_tensor(row[:, 2, :], row[:, 1, :], pad_row[:], ALU.mult))
            link(dve.scalar_tensor_tensor(y_row[:], row[:, 0, :], float(-B * P), row[:, 2, :], ALU.add, ALU.add))
            link(dve.tensor_scalar(row[:, 3, :], codes, float(2 * B), float(-B * P), ALU.is_ge, ALU.mult))
            link(dve.tensor_tensor(row[:, 3, :], row[:, 3, :], row[:, 0, :], ALU.add))
            link(dve.tensor_scalar(gather_row[:], row[:, 3, :], float(-B * P), 0.0, ALU.add, ALU.max))

            dve.wait_ge(gap_exp, 1)
            link(dve.tensor_scalar(gate[:, 1, :], gap[:], 1.0, None, ALU.add))
            link(dve.reciprocal(gate[:, 0, :], gate[:, 1, :]))
            link(dve.tensor_tensor(gate[:, 1, :], gap[:], gate[:, 0, :], ALU.mult))

            def step(q, r, has):
                if has(0):
                    j, e, turn = slot(q, r, 0)
                    wait(dve, gathered[e], turn * 16)
                    dve.tensor_copy(gidx[e][:], gather_row[:, bass.ds(j, 1)]).then_inc(gidx_set, 1)
                if has(6):
                    j, e, turn = slot(q, r, 6)
                    wait(dve, scattered[e], turn * 16)
                    dve.tensor_copy(yidx[e][:], y_row[:, bass.ds(j, 1)]).then_inc(yidx_set, 1)
                if has(3):
                    j, e, turn = slot(q, r, 3)
                    dve.wait_ge(gT_high, j + 1)
                    dve.tensor_tensor(xg_lo[:, e % 2], bank[e % 2][:, 0:P], xg_hi[:, e % 2].bitcast(F32), ALU.subtract
                                      ).then_inc(gT_low, 1)
                if has(5):
                    j, e, turn = slot(q, r, 5)
                    dve.wait_ge(hT_high, j + 1)
                    dve.tensor_tensor(hT_lo[:, e % 2], bank[4 + e % 2][:], hT_hi[:, e % 2].bitcast(F32), ALU.subtract
                                      ).then_inc(hT_low_done, 1)
                if has(6):
                    j, e, turn = slot(q, r, 6)
                    dve.wait_ge(y_done, j + 1)
                    dve.tensor_reduce(y_sb[e], bank[6 + e % 2][:, 0:2 * D].rearrange("p (a d) -> p d a", a=2),
                                      AX.X, ALU.add).then_inc(y_copied, 1)
            slot_steps(dve, step)

            with dve.Fori(0, NB // 2) as q:
                for r in range(2):
                    j = q * 2 + r
                    for k, loaded, added in ((0, y0_in, first_added), (1, y1_in, both_added)):
                        dve.wait_ge(loaded[r], q * 16 + 16)
                        for g in range(G):
                            row_x = x_all[:, bass.ds(j * G + g, 1), :].rearrange("p o d -> p (o d)")
                            last = dve.scalar_tensor_tensor(row_x, y_in[k][:, r, g, :], gate[:, k, bass.ds(j * G + g, 1)], row_x,
                                                            ALU.mult, ALU.add)
                        last.then_inc(added, 1)
                        if k == 0:
                            dve.wait_ge(added, j + 1)

        @block.tensor
        def _(pe):
            pe.wait_ge(made_c, 1)
            pe.wait_ge(const_in, 80)
            pe.transpose(bank[0][:, 0:P], w_gat[:], ident[:]).then_inc(wT_done, 1)
            pe.wait_ge(wT_copied, 1)
            pe.wait_ge(a_summed, 1)
            pe.matmul(bank[1][:, 0:1], w_gatT[:], a_sum[:], start=True, stop=True).then_inc(ws_done, 1)
            pe.wait_ge(ws_copied, 1)

            def step(q, r, has):
                if has(1):
                    j, e, turn = batch(q, r, 1)
                    pe.wait_ge(normed, j + 1)
                    wait(pe, soft_step, (j - 1) * SOFT + 1)
                    for g in range(G):
                        last = pe.transpose(bank[0][:, g * N:(g + 1) * N], xn[:, e, g, :], ident[:])
                    last.then_inc(xT_done, 1)
                if has(4):
                    j, e, turn = batch(q, r, 4)
                    pe.wait_ge(normed2, j + 1)
                    wait(pe, logit_copied, j)
                    for g in range(G):
                        last = pe.transpose(bank[2][:, g * N:(g + 1) * N], xn2[:, e, g, :], ident[:])
                    last.then_inc(x2T_done, 1)
                if has(1):
                    j, e, turn = batch(q, r, 1)
                    pe.wait_ge(xT_copied, j + 1)
                    wait(pe, h_copied, j - 1)
                    for g in range(G):
                        pe.matmul(bank[3 + e][:, g * D:(g + 1) * D], xnT[:, g, :], w_gat[:], start=True, stop=True)
                        last = pe.matmul(bank[0][:, g:g + 1], xnT[:, g, :], w_score[:], start=True, stop=True)
                    last.then_inc(h_done, 1)
                if has(4):
                    j, e, turn = batch(q, r, 4)
                    pe.wait_ge(x2T_copied, j + 1)
                    for g in range(G):
                        last = pe.matmul(bank[2][:, g * E:(g + 1) * E], xn2T[:, g, :], w_gate[:], start=True, stop=True)
                    last.then_inc(logit_done, 1)
                if has(2):
                    j, e, turn = batch(q, r, 2)
                    pe.wait_ge(att_done, j + 1)
                    wait(pe, aT_copied, j)
                    for g in range(G):
                        last = pe.transpose(bank[1][:, g * N:(g + 1) * N], att[:, g, :], ident[:])
                    last.then_inc(aT_done, 1)
                    pe.wait_ge(aT_copied, j + 1)
                    pe.wait_ge(h_copied, j + 1)
                    wait(pe, x2_done, j - 1)
                    for g in range(G):
                        last = pe.matmul(bank[5 + e][:, g * D:(g + 1) * D], attT[:, g, :], h_sb[:, e, g, :], start=True, stop=True)
                    last.then_inc(u_done, 1)

            attention_steps(pe, step)

            pe.wait_ge(totals, 1)
            pe.matmul(bank[7][:, 0:E], lower[:], upto[:, :, B - 1], start=True, stop=True)
            pe.matmul(bank[7][:, 8:8 + E], ones[:], upto[:, :, B - 1], start=True, stop=True).then_inc(counts, 1)

            def hot(n, r, first, last):
                pe.wait_ge(hot_coded, n + 1)
                pe.wait_ge(hot_scaled, n + 1)
                for g in range(QUAD):
                    mm = pe.matmul(bank[0][:, 0:2 * SLOTS], hot_q[:, r, :, g], hot_sv[:, r].rearrange("p a s g -> p (a s) g")[:, :, g],
                                   start=first and g == 0, stop=last and g == QUAD - 1)
                mm.then_inc(hot_used, 1)
            hot_steps(pe, hot)

            pe.wait_ge(experts_known, 1)
            pe.wait_ge(w_low, NB)
            pe.wait_ge(b_joined, 16)
            pe.wait_ge(found_copied, 1)

            expert_reg = [pe.alloc_register(f"expert{i}") for i in range(4)]

            def expert_in(e):
                return pe.snap(expert_reg[e], min_val=0, max_val=E - 1)

            def step(q, r, has):
                if r % 2 == 0 and has(4):
                    j, e, turn = slot(q, r, 4)
                    pe.load(expert_reg[e:e + 2], slot_expert[0:1, bass.ds(j, 2)])
                if has(3):
                    j, e, turn = slot(q, r, 3)
                    pe.wait_ge(gathered[e], turn * 16 + 16)
                    wait(pe, gT_low, j - 1)
                    pe.transpose(bank[e % 2][:, 0:P], xg[e], ident[:]).then_inc(gT_done, 1)
                if has(4):
                    j, e, turn = slot(q, r, 4)
                    expert = expert_in(e)
                    wait(pe, gelu_done, j - 1)
                    pre = bank[2 + e % 2][:]
                    pe.matmul(pre, ones_r[:], b1_hl[:, bass.ds(expert, 1), :], start=True, stop=False)
                    pe.wait_ge(gT_low, j + 1)
                    pe.matmul(pre, xg_hi[:, e % 2], w1_hi[:, bass.ds(expert, 1), :], start=False, stop=False)
                    pe.matmul(pre, xg_hi[:, e % 2], w1_lo[:, bass.ds(expert, 1), :], start=False, stop=False)
                    pe.matmul(pre, xg_lo[:, e % 2], w1_hi[:, bass.ds(expert, 1), :], start=False, stop=True).then_inc(pre_done, 1)
                if has(5):
                    j, e, turn = slot(q, r, 5)
                    pe.wait_ge(gelu_done, j + 1)
                    wait(pe, hT_low_done, j - 1)
                    for c in range(C):
                        last = pe.transpose(bank[4 + e % 2][:, c * P:(c + 1) * P], act_h[:, e % 2, c * P:(c + 1) * P], ident[:])
                    last.then_inc(hT_done, 1)
                if has(6):
                    j, e, turn = slot(q, r, 6)
                    expert = expert_in(e)
                    wait(pe, y_copied, j - 1)
                    y = bank[6 + e % 2]
                    pe.wait_ge(hT_low_done, j + 1)
                    for c in range(C):
                        pe.matmul(y[:, 0:2 * D], hT_hi[:, e % 2, c * P:(c + 1) * P],
                                  w2_hl[:, bass.ds(expert, 1), c, :, :], start=(c == 0), stop=False)
                        pe.matmul(y[:, 0:D], hT_lo[:, e % 2, c * P:(c + 1) * P],
                                  w2_hl[:, bass.ds(expert, 1), c, 0, :], start=False, stop=False)
                    pe.matmul(y[:, 0:D], ones_r[:], b2_hl[:, bass.ds(expert, 1), :], start=False, stop=True).then_inc(y_done, 1)
            slot_steps(pe, step)


_INS = ['x', 'adj', 'L0_gnn_W', 'L0_gnn_a', 'L0_ffn_Wg', 'L0_ffn_bg', 'L0_ffn_W1', 'L0_ffn_b1', 'L0_ffn_W2', 'L0_ffn_b2']


def kernel(**inputs):
    import numpy as _np
    import concourse.bacc as _bacc
    from concourse import mybir as _mybir
    from concourse.bass_utils import run_bass_kernel_spmd as _run

    nc = _bacc.Bacc("TRN2", target_bir_lowering=False, num_devices=1)
    arrays, args = {}, []
    for name in _INS:
        a = _np.ascontiguousarray(inputs[name])
        arrays[f"in_{name}_dram"] = a
        args.append(nc.dram_tensor(f"in_{name}_dram", a.shape, _mybir.dt.from_np(a.dtype), kind="ExternalInput").ap())
    shape = inputs['x'].shape
    args.append(nc.dram_tensor("out_0_dram", shape, _mybir.dt.float32, kind="ExternalOutput").ap())
    gat_moe(nc, *args)
    r = _run(nc, [arrays], core_ids=[0])
    return r.results[0]["out_0_dram"]
```

```python
from contextlib import ExitStack

import concourse.bass as bass
from concourse import mybir

ALU = mybir.AluOpType
ACT = mybir.ActivationFunctionType
AX = mybir.AxisListType
F32 = mybir.dt.float32
F32R = mybir.dt.float32r
BF16 = mybir.dt.bfloat16
I32 = mybir.dt.int32

P = 128
ALPHA = 0.2
NEG = -9000000000000000.0
EPS = 1e-5
LOW = -3.0e38


def gat_moe(nc, x, adj, W, a, Wg, bg, W1, b1, W2, b2, out):
    B, N, D = x.shape
    E, _, H = W1.shape
    T = B * N
    G = 4
    NB = B // G
    C = H // P
    K = 2
    RUN = T * K // P + E - 1
    SLOTS = -(-RUN // 8) * 8
    assert N == P and D == P and K * B == P and B % (4 * G) == 0 and SLOTS <= 256 and B * (K + 1) <= 256

    x_dram = x.rearrange("(b g) n d -> b n g d", g=G)
    adj_dram = adj.rearrange("(b g) n d -> b n g d", g=G)
    out_dram = out.rearrange("(b g) n d -> b n g d", g=G)

    with ExitStack() as ctx:
        def sb(name, shape, dt=F32):
            return ctx.enter_context(nc.sbuf_tensor(name, shape, dt))

        def sem(name):
            return ctx.enter_context(nc.semaphore(name))

        tok_dram = nc.dram_tensor("tok_dram", (T, D), F32, kind="Internal").ap()
        y_dram = nc.dram_tensor("y_dram", (K * T + SLOTS * P, D), F32, kind="Internal").ap()
        b_dram = nc.dram_tensor("b_dram", (2, E * D), F32R, kind="Internal").ap()
        tok_store = tok_dram.rearrange("(b g n) d -> b n g d", g=G, n=N)
        y_load = y_dram[0:K * T, :].rearrange("(k b g n) d -> b k n g d", k=K, g=G, n=N)

        bank = [ctx.enter_context(nc.psum_tensor(f"bank{i}", [P, 512], F32)) for i in range(8)]

        ident = sb("ident", [P, P])
        ones = sb("ones", [P, P])
        lower = sb("lower", [P, P])
        ones_r = sb("ones_r", [2, P], F32R)
        w_gat_s = sb("w_gat_s", [P, D + 1])
        w_gat = w_gat_s[:, 0:D]
        w_gatT = sb("w_gatT", [D, P])
        a_both = sb("a_both", [D, 2])
        a_sum = sb("a_sum", [D, 1])
        w_gate = sb("w_gate", [P, E])
        b_gate = sb("b_gate", [P, E])
        HALF = H // 2
        w_raw = sb("w_raw", [P, 2, 2, HALF])
        w1_hi = sb("w1_hi", [P, E, H], F32R)
        w1_lo = sb("w1_lo", [P, E, H], F32R)
        w2_hl = sb("w2_hl", [P, E, C, 2, D], F32R)
        b1_wide = sb("b1_wide", [P, E, H])
        b_raw = sb("b_raw", [E, D])
        b_high = sb("b_high", [E, D], F32R)
        b_low = sb("b_low", [E, D], F32R)
        b2_hl = sb("b2_hl", [2, E, D], F32R)

        x_all = sb("x_all", [P, B, D])
        x_ring = sb("x_ring", [P, 2, G, D])
        x2_ring = sb("x2_ring", [P, 2, G, D])
        adj_ring = sb("adj_ring", [P, 2, G, N])
        mask = sb("mask", [P, 2, G, N])
        stats = sb("stats", [P, G, 6])
        mv = sb("mv", [P, 2, G, 2])
        rstd = sb("rstd", [P, 2, G])
        stats2 = sb("stats2", [P, G, 6])
        mv2 = sb("mv2", [P, 2, G, 2])
        rstd2 = sb("rstd2", [P, 2, G])
        back = sb("back", [P, 2, G])
        back2 = sb("back2", [P, 2, G])
        eps = sb("eps", [P, G])
        half = sb("half", [P, G])
        minus1 = sb("minus1", [P, G])
        xn = sb("xn", [P, 2, G, D])
        xnT = sb("xnT", [P, G, N])
        h_sb = sb("h_sb", [P, 2, G, D + 1])
        edges = sb("edges", [P, 2, 2, G])
        alone = sb("alone", [P, 2, 2, G])
        leaky = sb("leaky", [P, G])
        shift = sb("shift", [P, 2, G])
        expo = sb("expo", [P, 2, G])
        weigh = sb("weigh", [P, 5, G])
        att_a = sb("att_a", [P, G])
        att_b = sb("att_b", [P, G])
        act_h = sb("act_h", [P, 2, H])
        att = act_h[:, 0, :].rearrange("p (g n) -> p g n", g=G)
        attT = act_h[:, 1, :].rearrange("p (g n) -> p g n", g=G)
        exp_u = sb("exp_u", [P, G, D])
        xe = sb("xe", [P, G, D])
        x_less1 = sb("x_less1", [P, G, D])
        xn2 = sb("xn2", [P, 2, G, D])
        xn2T = sb("xn2T", [P, G, N])
        logits = sb("logits", [P, B, E])

        GROUPS = K * B
        rev = sb("rev", [P, E])
        iota_i = sb("iota_i", [P, P + SLOTS], I32)
        rev_i = sb("rev_i", [P, E], I32)
        node_i = sb("node_i", [P, 1], I32)
        slot_i = sb("slot_i", [P, SLOTS], I32)
        QUAD = 4
        iota_q = sb("iota_q", [P, P, QUAD], BF16)
        iota_s = sb("iota_s", [P, SLOTS, QUAD], BF16)
        iota_sf = sb("iota_sf", [1, SLOTS])
        code = sb("code", [P, GROUPS], BF16)
        node = sb("node", [P, 1])
        pad_row = sb("pad_row", [P, SLOTS])
        reset = sb("reset", [P, E, B])
        first = sb("first", [P, 2, B])
        work = [mask[:, i].rearrange("p g n -> p (g n)").rearrange("p (b e) -> p b e", b=B) for i in range(2)]
        key = sb("key", [P, K, B])
        chosen = xn[:].rearrange("p k g d -> p (k g d)").rearrange("p (k b e) -> p k b e", k=K, b=B)
        member, upto = [h_sb[:, i].rearrange("p g d -> p (g d)")[:, 0:E * B].rearrange("p (e b) -> p e b", e=E) for i in range(2)]
        rows = sb("rows", [P, 6, E])
        rows_i = sb("rows_i", [P, 2, E], I32)
        pos = sb("pos", [P, GROUPS])
        pos_i = sb("pos_i", [P, 3, GROUPS], I32)
        pos_q = sb("pos_q", [P, GROUPS], BF16)
        pos_s = sb("pos_s", [P, GROUPS], BF16)
        gap = sb("gap", [P, B])
        gate = sb("gate", [P, K, B])
        past = h_sb[0:1].rearrange("p k g d -> p (k g d)")[:, 0:(E - 1) * SLOTS].rearrange("p (e s) -> p e s", e=E - 1)
        slot_e = sb("slot_e", [1, SLOTS])
        slot_expert = sb("slot_expert", [1, SLOTS], I32)
        HOT = 4
        x_free = x_ring[:].bitcast(BF16).rearrange("p r g d -> p (r g d)")
        w_free = w_raw[:].bitcast(BF16).rearrange("p r k h -> p (r k h)")
        x2_free = x2_ring[:].bitcast(BF16).rearrange("p r g d -> p (r g d)")
        hot_q = [x2_free[:, i * P * QUAD:(i + 1) * P * QUAD].rearrange("p (c g) -> p c g", g=QUAD) for i in range(HOT)]
        hot_s = [t[:, i * SLOTS * QUAD:(i + 1) * SLOTS * QUAD].rearrange("p (s g) -> p s g", g=QUAD)
                 for t in (x_free, w_free) for i in range(2)]
        hot_sv = sb("hot_sv", [P, HOT, 2, SLOTS, QUAD], BF16)
        places = adj_ring[:].rearrange("p r g n -> p (r g n)")[:, 0:6 * SLOTS].rearrange("p (k s) -> p k s", k=6)
        found, row = places[:, 0:2, :], places[:, 2:6, :]
        gather_row = sb("gather_row", [P, SLOTS], I32)
        y_row = sb("y_row", [P, SLOTS], I32)

        gidx = [sb(f"gidx{i}", [P, 1], I32) for i in range(4)]
        yidx = [sb(f"yidx{i}", [P, 1], I32) for i in range(4)]
        xg = [x_less1[:, i, :] for i in range(4)]
        xg_hi = sb("xg_hi", [P, 2, P], F32R)
        xg_lo = sb("xg_lo", [P, 2, P], F32R)
        hT_hi = sb("hT_hi", [P, 2, H], F32R)
        hT_lo = sb("hT_lo", [P, 2, H], F32R)
        y_sb = [exp_u[:, i, :] for i in range(4)]
        AHEAD = 4
        y_in = [b1_wide[:, AHEAD * k:AHEAD * (k + 1), :].rearrange("p a (g d) -> p a g d", g=G) for k in range(K)]

        x_in = [sem(f"x_in{i}") for i in range(2)]
        ring_in = [sem(f"ring_in{i}") for i in range(2)]
        x2_kept = [sem(f"x2_kept{i}") for i in range(2)]
        adj_in = [sem(f"adj_in{i}") for i in range(2)]
        const_in, b_in, b1_in = sem("const_in"), sem("b_in"), sem("b1_in")
        w_in = [sem(f"w_in{i}") for i in range(4)]
        made, made_i, made_c = sem("made"), sem("made_i"), sem("made_c")
        ident_made, rev_made = sem("ident_made"), sem("rev_made")
        a_summed, wT_done, wT_copied, ws_done, ws_copied = (
            sem("a_summed"), sem("wT_done"), sem("wT_copied"), sem("ws_done"), sem("ws_copied"))
        w_high, w_low = sem("w_high"), sem("w_low")
        b_parted = [sem(f"b_parted{i}") for i in range(2)]
        b_high_made, b_low_made, b_joined = sem("b_high_made"), sem("b_low_made"), sem("b_joined")
        stat_step, rstd_step, normed = sem("stat_step"), sem("rstd_step"), sem("normed")
        xT_done, xT_copied = sem("xT_done"), sem("xT_copied")
        h_done, h_copied = sem("h_done"), sem("h_copied")
        mask_made, counted = sem("mask_made"), sem("counted")
        soft_step, soft_exp, att_done = sem("soft_step"), sem("soft_exp"), sem("att_done")
        aT_done, aT_copied = sem("aT_done"), sem("aT_copied")
        u_done, u_exp, x2_done = sem("u_done"), sem("u_exp"), sem("x2_done")
        stat2_step, rstd2_step, normed2 = sem("stat2_step"), sem("rstd2_step"), sem("normed2")
        x2T_done, x2T_copied = sem("x2T_done"), sem("x2T_copied")
        logit_done, logit_copied = sem("logit_done"), sem("logit_copied")
        tok_out = [sem(f"tok_out{i}") for i in range(2)]
        tokens_stored = sem("tokens_stored")
        route = sem("route")
        totals, counts = sem("totals"), sem("counts")
        gap_made, gap_exp = sem("gap_made"), sem("gap_exp")
        pos_made = sem("pos_made")
        hot_coded = [sem(f"hot_coded{i}") for i in range(2)]
        hot_used, hot_q_made = sem("hot_used"), sem("hot_q_made")
        hot_made, hot_scaled = sem("hot_made"), sem("hot_scaled")
        back_made, back2_made = sem("back_made"), sem("back2_made")
        elu_made, less1_made = sem("elu_made"), sem("less1_made")
        found_copied = sem("found_copied")
        experts_known = sem("experts_known")
        gidx_set, yidx_set = sem("gidx_set"), sem("yidx_set")
        gathered = [sem(f"gathered{i}") for i in range(4)]
        scattered = [sem(f"scattered{i}") for i in range(4)]
        gT_done, gT_high, gT_low = sem("gT_done"), sem("gT_high"), sem("gT_low")
        pre_done, gelu_done = sem("pre_done"), sem("gelu_done")
        biased = sem("biased")
        hT_done, hT_high, hT_low_done = sem("hT_done"), sem("hT_high"), sem("hT_low_done")
        y_done, y_copied = sem("y_done"), sem("y_copied")
        y_rows_in = [[sem(f"y{k}_in{i}") for i in range(AHEAD)] for k in range(K)]
        gates_made, y1_gated = sem("gates_made"), sem("y1_gated")
        first_added, both_added = sem("first_added"), sem("both_added")
        out_sent = [sem(f"out_sent{i}") for i in range(AHEAD)]

        HEAD, SOFT = 3, 10

        def attention_steps(eng, step, before_last=None):
            def at(i):
                step(i // 2, i % 2, lambda k: 0 <= i - k < NB)
            for i in range(8):
                at(i)
            with eng.Fori(2, NB // 4) as q:
                for r in range(4):
                    step(q * 2 + r // 2, r % 2, lambda k: True)
            for i in range(NB, NB + 4):
                at(i)
            if before_last:
                before_last()
            for i in range(NB + 4, NB + 6):
                at(i)

        def batch(q, r, k):
            e = (r - k) % 2
            turn = q + (r - k - e) // 2
            return turn * 2 + e, e, turn

        def slot_steps(eng, step, after_three=None):
            def at(i):
                step(i // 8, i % 8, lambda k: 0 <= i - k < RUN)
            for i in range(8):
                at(i)
                if i == 2 and after_three:
                    after_three()
            with eng.Fori(1, RUN // 8) as q:
                for r in range(8):
                    step(q, r, lambda k: True)
            for i in range(RUN // 8 * 8, RUN + 8):
                at(i)

        def slot(q, r, k):
            m = (r - k) % 8
            octet = q + (r - k - m) // 8
            return octet * 8 + m, m % 4, octet * 2 + m // 4

        def hot_steps(eng, step):
            turns = GROUPS // QUAD // HOT
            for r in range(HOT):
                step(0, r, r == 0, False)
            with eng.Fori(1, turns - 1) as q:
                for r in range(HOT):
                    step(q, r, False, False)
            for r in range(HOT):
                step(turns - 1, r, False, r == HOT - 1)

        def groups_of(t, n, width):
            return t[:, bass.ds(n * QUAD, QUAD)].unsqueeze(1).to_broadcast([P, width, QUAD])

        def times_code(eng, q, r):
            n = q * HOT + r
            eng.wait_ge(hot_made, n + 1)
            eng.tensor_tensor(hot_sv[:, r, 0], hot_s[r], groups_of(code, n, SLOTS), ALU.mult).then_inc(hot_coded[r % 2], 1)

        def wait(eng, semaphore, value):
            if not isinstance(value, int) or value > 0:
                eng.wait_ge(semaphore, value)

        def expert_of(t, e):
            return t[bass.ds(e, 1)].rearrange("o a b -> (o a) b")

        def one(t, e):
            v = t[:, bass.ds(e, 1)]
            return v.rearrange("p o h -> p (o h)") if len(v.shape) == 3 else v.rearrange("p o c k d -> p (o c) k d")

        def flat(ap):
            return ap.rearrange("p g d -> p (g d)")

        def some(t, j):
            return t[:, bass.ds(j * G, G), :]

        def dram(t, j):
            return t[bass.ds(j, 1)].rearrange("o n g d -> (o n) g d")

        block = ctx.enter_context(nc.Block())

        @block.sync
        def _(sp):
            def load(q, r, has):
                if has(0):
                    j, e, turn = batch(q, r, 0)
                    wait(sp, normed, j - 1)
                    sp.dma_start(x_ring[:, e], dram(x_dram, j)).then_inc(ring_in[e], 16)
                if has(5):
                    j, e, turn = batch(q, r, 5)
                    sp.wait_ge(normed2, j + 1)
                    sp.dma_start(dram(tok_store, j), xn2[:, e]).then_inc(tok_out[e], 16)
                    sp.dma_start(some(x_all, j), x2_ring[:, e]).then_inc(x2_kept[e], 16)
                if has(0):
                    j, e, turn = batch(q, r, 0)
                    wait(sp, x_in[e], turn * 16)
                    sp.dma_start(some(x_all, j), dram(x_dram, j)).then_inc(x_in[e], 16)
                    wait(sp, mask_made, j - 1)
                    sp.dma_start(adj_ring[:, e], dram(adj_dram, j)).then_inc(adj_in[e], 16)
                if has(0):
                    wait(sp, w_low, j - 1)
                    sp.dma_start(w_raw[:, e, 0, :], expert_of(W1, turn)[:, e * HALF:(e + 1) * HALF]
                                 ).then_inc(w_in[e], 16)
                    sp.dma_start(w_raw[:, e, 1, :].rearrange("p (c d) -> p c d", d=D),
                                 expert_of(W2, turn).rearrange("(c p) d -> p c d", p=P)[:, e * C // 2:(e + 1) * C // 2, :]
                                 ).then_inc(w_in[2 + e], 16)

            sp.dma_start(w_gat, W).then_inc(const_in, 16)
            for t in range(2):
                sp.dma_start(a_both[:, t:t + 1], a[t * D:(t + 1) * D, :]).then_inc(const_in, 16)
            sp.dma_start(w_gate[:], Wg).then_inc(const_in, 16)
            sp.dma_start(b_gate[:], bg.partition_broadcast(P)).then_inc(const_in, 16)
            attention_steps(sp, load)
            sp.dma_start(b1_wide[:].rearrange("p e h -> p (e h)"), b1.rearrange("e h -> (e h)").partition_broadcast(P)
                         ).then_inc(b1_in, 16)

            for e in range(2):
                sp.wait_ge(tok_out[e], 16 * NB // 2)
            sp.sem_inc(tokens_stored, 1)

            for e in range(4):
                sp.wait_ge(scattered[e], 16 * len(range(e, RUN, 4)))
            def fetch(q, r):
                for k in range(K):
                    sp.dma_start(y_in[k][:, r], y_load[bass.ds(q * AHEAD + r, 1), k].rearrange("o n g d -> (o n) g d")
                                 ).then_inc(y_rows_in[k][r], 16)
            def send(q, r, more):
                j = q * AHEAD + r
                sp.wait_ge(both_added, j + 1)
                if more:
                    fetch(q + 1, r)
                wait(sp, out_sent[r], q * 16)
                sp.dma_start(dram(out_dram, j), some(x_all, j)).then_inc(out_sent[r], 16)
            for r in range(AHEAD):
                fetch(0, r)
            for r in range(AHEAD):
                send(0, r, True)
            with sp.Fori(1, NB // AHEAD - 1) as q:
                for r in range(AHEAD):
                    send(q, r, True)
            for r in range(AHEAD):
                send(NB // AHEAD - 1, r, False)
            for r in range(AHEAD):
                sp.wait_ge(out_sent[r], 16 * NB // AHEAD)

        @block.gpsimd
        def _(pool):
            pool.memset(ident[:], 0.0).then_inc(made_i, 1)
            pool.wait_ge(made_i, 1)
            pool.affine_select(out=ident[:], in_=ident[:], compare_op=ALU.not_equal, fill=1.0, base=0,
                               pattern=[[-1, P]], channel_multiplier=1).then_inc(ident_made, 1)
            pool.memset(half[:], -0.5)
            pool.memset(minus1[:], -1.0)
            pool.memset(eps[:], EPS)
            pool.memset(ones[:], 1.0)
            pool.memset(lower[:], 1.0)
            pool.iota(rev_i[:], pattern=[[-1, E]], base=E, channel_multiplier=0).then_inc(made, 1)
            pool.wait_ge(made, 1)
            pool.tensor_copy(rev[:], rev_i[:]).then_inc(rev_made, 1)

            def step(q, r, has):
                if has(0):
                    j, e, turn = batch(q, r, 0)
                    wait(pool, normed, j - 1)
                    pool.wait_ge(stat_step, 2 * j + 2)
                    pool.nop(nofuse=True)
                    pool.tensor_tensor(mv[:, e, :, 1], mv[:, e, :, 1], eps[:], ALU.add).then_inc(rstd_step, 1)
                    pool.tensor_tensor(back[:, e, :], mv[:, e, :, 0], minus1[:], ALU.mult)
                    pool.wait_ge(rstd_step, 2 * j + 1)
                    pool.tensor_tensor(rstd[:, e, :], mv[:, e, :, 1], half[:], ALU.pow).then_inc(rstd_step, 1)
                    pool.wait_ge(rstd_step, 2 * j + 2)
                    pool.tensor_tensor(back[:, e, :], back[:, e, :], rstd[:, e, :], ALU.mult).then_inc(back_made, 1)
                if has(2):
                    j, e, turn = batch(q, r, 2)
                    pool.wait_ge(x_in[e], turn * 16 + 16)
                    wait(pool, elu_made, j)
                    pool.tensor_tensor(x_less1[:], some(x_all, j), minus1[:, 0:1].unsqueeze(2).to_broadcast([P, G, D]),
                                       ALU.add).then_inc(less1_made, 1)
                if has(3):
                    j, e, turn = batch(q, r, 3)
                    wait(pool, normed2, j - 1)
                    pool.wait_ge(stat2_step, 2 * j + 2)
                    pool.tensor_tensor(mv2[:, e, :, 1], mv2[:, e, :, 1], eps[:], ALU.add).then_inc(rstd2_step, 1)
                    pool.tensor_tensor(back2[:, e, :], mv2[:, e, :, 0], minus1[:], ALU.mult)
                    pool.wait_ge(rstd2_step, 2 * j + 1)
                    pool.tensor_tensor(rstd2[:, e, :], mv2[:, e, :, 1], half[:], ALU.pow).then_inc(rstd2_step, 1)
                    pool.wait_ge(rstd2_step, 2 * j + 2)
                    pool.tensor_tensor(back2[:, e, :], back2[:, e, :], rstd2[:, e, :], ALU.mult).then_inc(back2_made, 1)
                if has(1):
                    j, e, turn = batch(q, r, 1)
                    pool.wait_ge(w_high, j + 1)
                    w1_part = slice(e * HALF, (e + 1) * HALF)
                    w2_part = slice(e * C // 2, (e + 1) * C // 2)
                    pool.tensor_tensor(one(w1_lo, turn)[:, w1_part], w_raw[:, e, 0, :],
                                       one(w1_hi, turn)[:, w1_part].bitcast(F32), ALU.subtract)
                    pool.tensor_tensor(one(w2_hl, turn)[:, w2_part, 1, :], w_raw[:, e, 1, :].rearrange("p (c d) -> p c d", d=D),
                                       one(w2_hl, turn)[:, w2_part, 0, :].bitcast(F32), ALU.subtract).then_inc(w_low, 1)

            attention_steps(pool, step)

            pool.iota(iota_q[:], pattern=[[1, P], [0, QUAD]], base=0, channel_multiplier=0,
                      allow_small_or_imprecise_dtypes=True)
            pool.iota(iota_s[:], pattern=[[1, SLOTS], [0, QUAD]], base=0, channel_multiplier=0,
                      allow_small_or_imprecise_dtypes=True)
            pool.memset(ones_r[:].bitcast(F32), 1.0)
            pool.memset(reset[:], 1.0)
            pool.iota(iota_i[:, 0:SLOTS], pattern=[[P, SLOTS]], base=K * T + B * P, channel_multiplier=1)
            pool.iota(iota_i[:, SLOTS:SLOTS + P], pattern=[[1, P]], base=B, channel_multiplier=0)
            pool.affine_select(out=lower[:], in_=lower[:], compare_op=ALU.is_ge, fill=0.0, base=-1,
                               pattern=[[1, P]], channel_multiplier=-1)
            pool.iota(node_i[:], pattern=[[1, 1]], base=0, channel_multiplier=1)
            pool.iota(slot_i[:], pattern=[[1, SLOTS]], base=0, channel_multiplier=0).then_inc(made, 1)
            pool.wait_ge(made, 2)
            pool.memset(reset[:, :, 0:1], 0.0)
            for dst, src in ((iota_sf[:], slot_i[0:1, :]), (node[:], node_i[:]),
                             (pad_row[:], iota_i[:, 0:SLOTS]), (code[:], iota_i[:, SLOTS:SLOTS + P])):
                last = pool.tensor_copy(dst, src)
            last.then_inc(made_c, 1)

            pool.wait_ge(b_high_made, 1)
            pool.tensor_tensor(b_low[:], b_raw[:], b_high[:].bitcast(F32), ALU.subtract).then_inc(b_low_made, 1)
            pool.wait_ge(b_low_made, 1)
            pool.dma_start(b_dram[0].rearrange("(e d) -> e d", d=D), b_high[:]).then_inc(b_parted[0], 16)
            pool.dma_start(b_dram[1].rearrange("(e d) -> e d", d=D), b_low[:]).then_inc(b_parted[1], 16)
            pool.wait_ge(b_parted[0], 16)
            pool.wait_ge(b_parted[1], 16)
            pool.dma_start(b2_hl[:].rearrange("p e d -> p (e d)"), b_dram).then_inc(b_joined, 16)

            pool.wait_ge(pos_made, 1)
            def hot(q, r, first, last):
                if r % 2 == 1:
                    times_code(pool, q, r)
            hot_steps(pool, hot)

            def step(q, r, has):
                if has(0):
                    j, e, turn = slot(q, r, 0)
                    pool.wait_ge(gidx_set, j + 1)
                    wait(pool, gT_done, j - 3)
                    pool.nop(nofuse=True)
                    pool.indirect_dma_start(xg[e], None, tok_dram, bass.IndirectOffsetOnAxis(ap=gidx[e][:], axis=0)
                                            ).then_inc(gathered[e], 16)
                if has(8):
                    j, e, turn = slot(q, r, 8)
                    pool.wait_ge(yidx_set, j + 1)
                    pool.wait_ge(y_copied, j + 1)
                    pool.nop(nofuse=True)
                    pool.indirect_dma_start(y_dram, bass.IndirectOffsetOnAxis(ap=yidx[e][:], axis=0), y_sb[e], None
                                            ).then_inc(scattered[e], 16)
            pool.wait_ge(tokens_stored, 1)
            slot_steps(pool, step)

            with pool.Fori(0, NB // AHEAD) as q:
                for r in range(AHEAD):
                    j = q * AHEAD + r
                    pool.wait_ge(first_added, j + 1)
                    pool.wait_ge(y1_gated, j + 1)
                    pool.tensor_tensor(some(x_all, j), some(x_all, j), y_in[1][:, r], ALU.add).then_inc(both_added, 1)

        @block.scalar
        def _(act):
            act.dma_start(b_raw[:], b2).then_inc(b_in, 16)
            act.wait_ge(wT_done, 1)
            act.activation(w_gatT[:], bank[0][:, 0:P], ACT.Copy).then_inc(wT_copied, 1)
            act.wait_ge(ws_done, 1)
            act.activation(w_gat_s[:, D:D + 1], bank[1][:, 0:1], ACT.Copy).then_inc(ws_copied, 1)

            def step(q, r, has):
                if has(2):
                    j, e, turn = batch(q, r, 2)
                    act.wait_ge(soft_step, j * SOFT + HEAD)
                    act.activation(expo[:, 0, :], shift[:, 0, :], ACT.Exp)
                    act.activation(expo[:, 1, :], shift[:, 1, :], ACT.Exp, scale=-1.0).then_inc(soft_exp, 1)
                if has(1):
                    j, e, turn = batch(q, r, 1)
                    act.wait_ge(back_made, j + 1)
                    wait(act, xT_done, j - 1)
                    for g in range(G):
                        last = act.activation(xn[:, e, g, :], x_ring[:, e, g, :], ACT.Identity,
                                              bias=back[:, e, g:g + 1], scale=rstd[:, e, g:g + 1])
                    last.then_inc(normed, 1)
                if has(3):
                    j, e, turn = batch(q, r, 3)
                    act.wait_ge(u_done, j + 1)
                    wait(act, elu_made, j)
                    act.activation(exp_u[:].rearrange("p g d -> p (g d)"), bank[5 + e][:], ACT.Exp).then_inc(u_exp, 1)
                if has(1):
                    j, e, turn = batch(q, r, 1)
                    act.wait_ge(xT_done, j + 1)
                    wait(act, h_done, j)
                    act.activation(xnT[:].rearrange("p g n -> p (g n)"), bank[0][:], ACT.Copy).then_inc(xT_copied, 1)
                if has(4):
                    j, e, turn = batch(q, r, 4)
                    act.wait_ge(back2_made, j + 1)
                    wait(act, x2T_done, j - 1)
                    wait(act, tok_out[e], turn * 16)
                    for g in range(G):
                        last = act.activation(xn2[:, e, g, :], x2_ring[:, e, g, :], ACT.Identity,
                                              bias=back2[:, e, g:g + 1], scale=rstd2[:, e, g:g + 1])
                    last.then_inc(normed2, 1)
                if has(2):
                    j, e, turn = batch(q, r, 2)
                    act.wait_ge(aT_done, j + 1)
                    wait(act, u_done, j)
                    act.activation(attT.rearrange("p g n -> p (g n)"), bank[1][:], ACT.Copy).then_inc(aT_copied, 1)
                if has(1):
                    j, e, turn = batch(q, r, 1)
                    act.wait_ge(h_done, j + 1)
                    wait(act, u_done, j - 1)
                    wait(act, soft_step, (j - 2) * SOFT + 1)
                    for b in range(2):
                        last = act.activation(h_sb[:, e, 2 * b:2 * b + 2, :], bank[3 + b][:, 0:2 * (D + 1)].rearrange(
                            "p (g d) -> p g d", g=2), ACT.Copy)
                    last.then_inc(h_copied, 1)
                if has(0):
                    j, e, turn = batch(q, r, 0)
                    act.wait_ge(w_in[e], turn * 16 + 16)
                    act.activation(one(w1_hi, turn)[:, e * HALF:(e + 1) * HALF], w_raw[:, e, 0, :], ACT.Copy)
                    act.wait_ge(w_in[2 + e], turn * 16 + 16)
                    act.activation(one(w2_hl, turn)[:, e * C // 2:(e + 1) * C // 2, 0, :],
                                   w_raw[:, e, 1, :].rearrange("p (c d) -> p c d", d=D), ACT.Copy).then_inc(w_high, 1)
                if has(4):
                    j, e, turn = batch(q, r, 4)
                    act.wait_ge(x2T_done, j + 1)
                    wait(act, logit_done, j)
                    act.activation(xn2T[:].rearrange("p g n -> p (g n)"), bank[2][:], ACT.Copy).then_inc(x2T_copied, 1)

            attention_steps(act, step)

            act.wait_ge(b_in, 16)
            act.activation(b_high[:], b_raw[:], ACT.Copy).then_inc(b_high_made, 1)

            act.wait_ge(gap_made, 1)
            act.activation(gap[:], gap[:], ACT.Exp).then_inc(gap_exp, 1)

            act.wait_ge(made_c, 1)
            def hot(q, r, first, last):
                n = q * HOT + r
                act.wait_ge(hot_made, n + 1)
                wait(act, hot_used, n - HOT + 1)
                act.activation(hot_sv[:, r, 1].rearrange("p s g -> p (s g)"), hot_s[r].rearrange("p s g -> p (s g)"),
                               ACT.Copy, scale=node[:]).then_inc(hot_scaled, 1)
            hot_steps(act, hot)
            act.wait_ge(hot_used, GROUPS // QUAD)
            act.activation(found.rearrange("p a s -> p (a s)"), bank[0][:, 0:2 * SLOTS], ACT.Copy).then_inc(found_copied, 1)

            def step(q, r, has):
                if has(6):
                    j, e, turn = slot(q, r, 6)
                    act.wait_ge(hT_done, j + 1)
                    wait(act, y_done, j - 1)
                    act.activation(hT_hi[:, e % 2], bank[4 + e % 2][:], ACT.Copy).then_inc(hT_high, 1)
                if has(3):
                    j, e, turn = slot(q, r, 3)
                    act.wait_ge(gT_done, j + 1)
                    wait(act, pre_done, j - 1)
                    act.activation(xg_hi[:, e % 2], bank[e % 2][:, 0:P], ACT.Copy).then_inc(gT_high, 1)
                if has(5):
                    j, e, turn = slot(q, r, 5)
                    act.wait_ge(biased, j + 1)
                    act.activation(act_h[:, e % 2], act_h[:, e % 2], ACT.Gelu).then_inc(gelu_done, 1)
            slot_steps(act, step)

            act.wait_ge(gates_made, 1)
            with act.Fori(0, NB // AHEAD) as q:
                for r in range(AHEAD):
                    j = q * AHEAD + r
                    act.wait_ge(y_rows_in[1][r], q * 16 + 16)
                    for g in range(G):
                        last = act.activation(y_in[1][:, r, g, :], y_in[1][:, r, g, :], ACT.Copy,
                                              scale=gate[:, 1, bass.ds(j * G + g, 1)])
                    last.then_inc(y1_gated, 1)

        @block.vector
        def _(dve):
            dve.wait_ge(const_in, 80)
            dve.tensor_tensor(a_sum[:], a_both[:, 0:1], a_both[:, 1:2], ALU.add).then_inc(a_summed, 1)

            def step(q, r, has):
                head, tail = [], []
                if has(2):
                    j2, e2, turn2 = batch(q, r, 2)
                    w = [weigh[:, k, :] for k in range(5)]
                    head = [
                        lambda: dve.scalar_tensor_tensor(leaky[:], h_sb[:, e2, :, D], ALPHA, h_sb[:, e2, :, D], ALU.mult, ALU.max),
                        lambda: dve.tensor_scalar(shift[:, 0, :], leaky[:], -NEG, 0.0, ALU.add, ALU.min),
                        lambda: dve.tensor_scalar(shift[:, 1, :], leaky[:], -NEG, 0.0, ALU.add, ALU.max),
                    ]
                    tail = [
                        (HEAD, lambda: dve.tensor_tensor(expo[:], expo[:], alone[:, e2], ALU.max)),
                        (HEAD + 1, lambda: dve.tensor_tensor(weigh[:, 0:2, :], expo[:], edges[:, e2], ALU.mult)),
                        (HEAD + 1, lambda: dve.tensor_tensor(w[4], expo[:, 0, :], expo[:, 1, :], ALU.subtract)),
                        (HEAD + 2, lambda: dve.tensor_tensor(w[2], w[0], w[1], ALU.add)),
                        (HEAD + 4, lambda: dve.reciprocal(w[3], w[2])),
                        (HEAD + 5, lambda: dve.tensor_tensor(att_b[:], expo[:, 1, :], w[3], ALU.mult)),
                        (HEAD + 5, lambda: dve.tensor_tensor(att_a[:], w[4], w[3], ALU.mult)),
                    ]
                if has(0):
                    j0, e0, turn0 = batch(q, r, 0)
                    dve.wait_ge(ring_in[e0], turn0 * 16 + 16)
                    dve.nop(nofuse=True)
                for n in range(4):
                    if has(0):
                        last = dve.bn_stats(stats[:, n, :], x_ring[:, e0, n, :])
                        if n == G - 1:
                            last.then_inc(stat_step, 1)
                    if n < len(head):
                        dve.wait_ge(*((h_copied, j2 + 1) if n == 0 else (soft_step, j2 * SOFT + 1)))
                        head[n]().then_inc(soft_step, 1)
                if has(0):
                    dve.wait_ge(stat_step, 2 * j0 + 1)
                    dve.nop(nofuse=True)
                for n in range(7):
                    if tail:
                        needs, instruction = tail[n]
                        if n == 0:
                            dve.wait_ge(soft_exp, j2 + 1)
                        else:
                            dve.wait_ge(soft_step, j2 * SOFT + needs)
                        instruction().then_inc(soft_step, 1)
                    if has(0) and n < G:
                        last = dve.bn_aggr(mv[:, e0, n, :], stats[:, n, :])
                        if n == G - 1:
                            last.then_inc(stat_step, 1)
                if has(2):
                    dve.wait_ge(soft_step, j2 * SOFT + SOFT)
                    wait(dve, aT_done, j2)
                    for g in range(G):
                        last = dve.tensor_scalar(att[:, g, :], mask[:, e2, g, :], att_a[:, g:g + 1], att_b[:, g:g + 1],
                                                 ALU.mult, ALU.add)
                    last.then_inc(att_done, 1)
                if has(5):
                    j5, e5, turn5 = batch(q, r, 5)
                    dve.wait_ge(logit_done, j5 + 1)
                    dve.tensor_tensor(some(logits, j5), bank[2][:, 0:G * E].rearrange("p (g e) -> p g e", g=G),
                                      b_gate[:].unsqueeze(1).to_broadcast([P, G, E]), ALU.add).then_inc(logit_copied, 1)
                if has(3):
                    j3, e3, turn3 = batch(q, r, 3)
                    dve.wait_ge(u_exp, j3 + 1)
                    dve.wait_ge(less1_made, j3 + 1)
                    dve.scalar_tensor_tensor(flat(xe[:]), flat(exp_u[:]), 1.0, flat(x_less1[:]), ALU.min, ALU.add
                                             ).then_inc(elu_made, 1)
                if has(0):
                    dve.wait_ge(adj_in[e0], turn0 * 16 + 16)
                    wait(dve, att_done, j0 - 1)
                    dve.tensor_scalar(mask[:, e0], adj_ring[:, e0], 0.0, None, ALU.is_gt).then_inc(mask_made, 1)
                if has(3):
                    dve.wait_ge(elu_made, j3 + 1)
                    wait(dve, x2_kept[e3], turn3 * 16)
                    wait(dve, normed2, j3 - 1)
                    dve.scalar_tensor_tensor(flat(x2_ring[:, e3]), bank[5 + e3][:], 0.0, flat(xe[:]), ALU.max, ALU.add
                                             ).then_inc(x2_done, 1)
                if has(0):
                    dve.wait_ge(mask_made, j0 + 1)
                    dve.tensor_reduce(edges[:, e0, 0, :], mask[:, e0], AX.X, ALU.add).then_inc(counted, 1)
                if has(3):
                    dve.wait_ge(x2_done, j3 + 1)
                    dve.nop(nofuse=True)
                    for g in range(G):
                        last = dve.bn_stats(stats2[:, g, :], x2_ring[:, e3, g, :])
                    last.then_inc(stat2_step, 1)
                if has(0):
                    dve.wait_ge(counted, 2 * j0 + 1)
                    dve.tensor_scalar(edges[:, e0, 1, :], edges[:, e0, 0, :], -1.0, float(N), ALU.mult, ALU.add).then_inc(counted, 1)
                if has(3):
                    dve.wait_ge(stat2_step, 2 * j3 + 1)
                    dve.nop(nofuse=True)
                    for g in range(G):
                        last = dve.bn_aggr(mv2[:, e3, g, :], stats2[:, g, :])
                    last.then_inc(stat2_step, 1)
                if has(0):
                    dve.wait_ge(counted, 2 * j0 + 2)
                    dve.tensor_scalar(alone[:, e0], edges[:, e0, ::-1, :], 0.0, None, ALU.is_equal)

            done = [0]

            def link(instruction):
                done[0] += 1
                instruction.then_inc(route, 1)
                dve.wait_ge(route, done[0])

            def top_two(start, end):
                graphs = slice(start, end)
                rev_all = rev[:].unsqueeze(1).to_broadcast([P, end - start, E])

                def over_experts(ap):
                    return ap.unsqueeze(2).to_broadcast([P, end - start, E])

                source = logits[:, graphs]
                for k in range(K):
                    link(dve.tensor_reduce(first[:, k, graphs], source, AX.X, ALU.max))
                    link(dve.tensor_tensor(work[0][:, graphs], source, over_experts(first[:, k, graphs]), ALU.is_ge))
                    link(dve.tensor_tensor(work[0][:, graphs], work[0][:, graphs], rev_all, ALU.mult))
                    link(dve.tensor_reduce(key[:, k, graphs], work[0][:, graphs], AX.X, ALU.max))
                    link(dve.tensor_tensor(chosen[:, k, graphs], over_experts(key[:, k, graphs]), rev_all, ALU.is_equal))
                    if k == 0:
                        link(dve.scalar_tensor_tensor(work[1][:, graphs], chosen[:, 0, graphs], LOW, logits[:, graphs],
                                                      ALU.mult, ALU.add))
                        source = work[1][:, graphs]

            def top_two_of_most():
                dve.wait_ge(rev_made, 1)
                dve.wait_ge(logit_copied, NB - 1)
                dve.wait_ge(xT_done, NB)
                top_two(0, B - G)

            attention_steps(dve, step, top_two_of_most)
            dve.wait_ge(logit_copied, NB)
            top_two(B - G, B)
            dve.tensor_tensor(gap[:], first[:, 1, :], first[:, 0, :], ALU.subtract).then_inc(gap_made, 1)

            dve.wait_ge(made_c, 1)
            link(dve.tensor_tensor(member, chosen[:, 0].rearrange("p b e -> p e b"), chosen[:, 1].rearrange("p b e -> p e b"), ALU.add))
            dve.tensor_tensor_scan(upto.rearrange("p e b -> p (e b)"), reset[:].rearrange("p e b -> p (e b)"),
                                   member.rearrange("p e b -> p (e b)"), 0.0, ALU.mult, ALU.add).then_inc(totals, 1)
            dve.wait_ge(totals, 1)
            dve.wait_ge(counts, 1)
            link(dve.tensor_scalar(rows_i[:, 0, :], bank[7][:, 8:8 + E], float(P - 1), None, ALU.add))
            link(dve.tensor_scalar(rows_i[:, 1, :], rows_i[:, 0, :], 7, None, ALU.logical_shift_right))
            link(dve.tensor_copy(rows[:, 0, :], rows_i[:, 1, :]))
            link(dve.tensor_tensor_scan(rows[:, 1, :], ones[:, 0:E], rows[:, 0, :], 0.0, ALU.mult, ALU.add))
            link(dve.tensor_tensor(rows[:, 2, :], rows[:, 1, :], rows[:, 0, :], ALU.subtract))
            link(dve.scalar_tensor_tensor(rows[:, 3, :], rows[:, 2, :], float(P), bank[7][:, 0:E], ALU.mult, ALU.add))
            link(dve.tensor_tensor(upto, upto, rows[:, 3, :].unsqueeze(2).to_broadcast([P, E, B]), ALU.add))
            link(dve.tensor_tensor(chosen, chosen, upto.rearrange("p e b -> p b e").unsqueeze(1).to_broadcast([P, K, B, E]), ALU.mult))
            link(dve.tensor_reduce(pos[:].rearrange("p (k b) -> p k b", k=K), chosen, AX.X, ALU.add))
            link(dve.tensor_scalar(pos_i[:, 0, :], pos[:], -1.0, None, ALU.add))
            link(dve.tensor_scalar(pos_i[:, 1, :], pos_i[:, 0, :], P - 1, None, ALU.bitwise_and))
            link(dve.tensor_scalar(pos_i[:, 2, :], pos_i[:, 0, :], 7, None, ALU.logical_shift_right))
            link(dve.tensor_copy(pos_q[:], pos_i[:, 1, :]))
            dve.tensor_copy(pos_s[:], pos_i[:, 2, :]).then_inc(pos_made, 1)
            dve.wait_ge(pos_made, 1)

            def hot(q, r, first, last):
                n = q * HOT + r
                wait(dve, hot_used, n - HOT + 1)
                dve.tensor_tensor(hot_s[r], iota_s[:], groups_of(pos_s, n, SLOTS), ALU.is_equal).then_inc(hot_made, 1)
                dve.tensor_tensor(hot_q[r], iota_q[:], groups_of(pos_q, n, P), ALU.is_equal).then_inc(hot_q_made, 1)
                if r % 2 == 0:
                    times_code(dve, q, r)
            for e in range(2):
                dve.wait_ge(x2_kept[e], 16 * NB // 2)
            dve.wait_ge(normed2, NB)
            dve.wait_ge(w_low, NB)
            dve.wait_ge(normed, NB)
            hot_steps(dve, hot)

            dve.wait_ge(gap_exp, 1)
            link(dve.tensor_scalar(gate[:, 1, :], gap[:], 1.0, None, ALU.add))
            link(dve.reciprocal(gate[:, 0, :], gate[:, 1, :]))
            dve.tensor_tensor(gate[:, 1, :], gap[:], gate[:, 0, :], ALU.mult).then_inc(gates_made, 1)

            dve.wait_ge(found_copied, 1)
            codes, nodes = found[:, 0, :], found[:, 1, :]
            link(dve.scalar_tensor_tensor(row[:, 0, :], codes, float(P), nodes, ALU.mult, ALU.add))
            link(dve.tensor_scalar(row[:, 3, :], codes, float(2 * B), float(-B * P), ALU.is_ge, ALU.mult))
            link(dve.tensor_tensor(row[:, 3, :], row[:, 3, :], row[:, 0, :], ALU.add))
            link(dve.tensor_scalar(gather_row[:], row[:, 3, :], float(-B * P), 0.0, ALU.add, ALU.max))

            def while_gathering():
                link(dve.tensor_scalar(row[:, 1, :], codes, 0.0, None, ALU.is_equal))
                link(dve.tensor_tensor(row[:, 2, :], row[:, 1, :], pad_row[:], ALU.mult))
                link(dve.scalar_tensor_tensor(y_row[:], row[:, 0, :], float(-B * P), row[:, 2, :], ALU.add, ALU.add))
                link(dve.tensor_tensor(past, iota_sf[:].unsqueeze(1).to_broadcast([1, E - 1, SLOTS]),
                                       rows[0:1, 1, 0:E - 1].unsqueeze(2).to_broadcast([1, E - 1, SLOTS]), ALU.is_ge))
                link(dve.tensor_reduce(slot_e[:], past.rearrange("p e s -> p s e"), AX.X, ALU.add))
                dve.tensor_copy(slot_expert[:], slot_e[:]).then_inc(experts_known, 1)
                dve.wait_ge(experts_known, 1)

            expert_reg = [dve.alloc_register(f"bias_of{i}") for i in range(4)]
            dve.wait_ge(b1_in, 16)

            def step(q, r, has):
                if has(0):
                    j, e, turn = slot(q, r, 0)
                    wait(dve, gathered[e], turn * 16)
                    dve.tensor_copy(gidx[e][:], gather_row[:, bass.ds(j, 1)]).then_inc(gidx_set, 1)
                if has(8):
                    j, e, turn = slot(q, r, 8)
                    wait(dve, scattered[e], turn * 16)
                    dve.tensor_copy(yidx[e][:], y_row[:, bass.ds(j, 1)]).then_inc(yidx_set, 1)
                if has(8):
                    j, e, turn = slot(q, r, 8)
                    dve.wait_ge(y_done, j + 1)
                    dve.tensor_reduce(y_sb[e], bank[6 + e % 2][:, 0:2 * D].rearrange("p (a d) -> p d a", a=2),
                                      AX.X, ALU.add).then_inc(y_copied, 1)
                if has(6):
                    j, e, turn = slot(q, r, 6)
                    dve.wait_ge(hT_high, j + 1)
                    dve.tensor_tensor(hT_lo[:, e % 2], bank[4 + e % 2][:], hT_hi[:, e % 2].bitcast(F32), ALU.subtract
                                      ).then_inc(hT_low_done, 1)
                if has(3):
                    j, e, turn = slot(q, r, 3)
                    dve.wait_ge(gT_high, j + 1)
                    dve.tensor_tensor(xg_lo[:, e % 2], bank[e % 2][:, 0:P], xg_hi[:, e % 2].bitcast(F32), ALU.subtract
                                      ).then_inc(gT_low, 1)
                if has(4):
                    j, e, turn = slot(q, r, 4)
                    expert = dve.snap(expert_reg[e], min_val=0, max_val=E - 1)
                    dve.wait_ge(pre_done, j + 1)
                    wait(dve, hT_done, j - 1)
                    dve.tensor_tensor(act_h[:, e % 2], bank[2 + e % 2][:],
                                      b1_wide[:, bass.ds(expert, 1), :].rearrange("p o h -> p (o h)"), ALU.add
                                      ).then_inc(biased, 1)
                if r % 4 == 3 and has(3):
                    j, e, turn = slot(q, r, 3)
                    dve.load(expert_reg[0:4], slot_expert[0:1, bass.ds(j, 4)])
            slot_steps(dve, step, while_gathering)

            with dve.Fori(0, NB // AHEAD) as q:
                for r in range(AHEAD):
                    j = q * AHEAD + r
                    dve.wait_ge(y_rows_in[0][r], q * 16 + 16)
                    for g in range(G):
                        row_x = x_all[:, bass.ds(j * G + g, 1), :].rearrange("p o d -> p (o d)")
                        last = dve.scalar_tensor_tensor(row_x, y_in[0][:, r, g, :], gate[:, 0, bass.ds(j * G + g, 1)], row_x,
                                                        ALU.mult, ALU.add)
                    last.then_inc(first_added, 1)

        @block.tensor
        def _(pe):
            pe.wait_ge(ident_made, 1)
            pe.wait_ge(const_in, 80)
            pe.transpose(bank[0][:, 0:P], w_gat, ident[:]).then_inc(wT_done, 1)
            pe.wait_ge(wT_copied, 1)
            pe.wait_ge(a_summed, 1)
            pe.matmul(bank[1][:, 0:1], w_gatT[:], a_sum[:], start=True, stop=True).then_inc(ws_done, 1)
            pe.wait_ge(ws_copied, 1)

            def step(q, r, has):
                if has(5):
                    j, e, turn = batch(q, r, 5)
                    pe.wait_ge(x2T_copied, j + 1)
                    for g in range(G):
                        last = pe.matmul(bank[2][:, g * E:(g + 1) * E], xn2T[:, g, :], w_gate[:], start=True, stop=True)
                    last.then_inc(logit_done, 1)
                if has(1):
                    j, e, turn = batch(q, r, 1)
                    pe.wait_ge(normed, j + 1)
                    wait(pe, xT_copied, j)
                    for g in range(G):
                        last = pe.transpose(bank[0][:, g * N:(g + 1) * N], xn[:, e, g, :], ident[:])
                    last.then_inc(xT_done, 1)
                if has(2):
                    j, e, turn = batch(q, r, 2)
                    pe.wait_ge(att_done, j + 1)
                    wait(pe, aT_copied, j)
                    for g in range(G):
                        last = pe.transpose(bank[1][:, g * N:(g + 1) * N], att[:, g, :], ident[:])
                    last.then_inc(aT_done, 1)
                if has(1):
                    j, e, turn = batch(q, r, 1)
                    pe.wait_ge(xT_copied, j + 1)
                    wait(pe, h_copied, j)
                    for g in range(G):
                        last = pe.matmul(bank[3 + g // 2][:, g % 2 * (D + 1):(g % 2 + 1) * (D + 1)], xnT[:, g, :], w_gat_s[:],
                                         start=True, stop=True)
                    last.then_inc(h_done, 1)
                if has(4):
                    j, e, turn = batch(q, r, 4)
                    pe.wait_ge(normed2, j + 1)
                    wait(pe, logit_copied, j)
                    for g in range(G):
                        last = pe.transpose(bank[2][:, g * N:(g + 1) * N], xn2[:, e, g, :], ident[:])
                    last.then_inc(x2T_done, 1)
                if has(2):
                    j, e, turn = batch(q, r, 2)
                    pe.wait_ge(aT_copied, j + 1)
                    pe.wait_ge(h_copied, j + 1)
                    wait(pe, x2_done, j - 1)
                    for g in range(G):
                        last = pe.matmul(bank[5 + e][:, g * D:(g + 1) * D], attT[:, g, :], h_sb[:, e, g, 0:D], start=True, stop=True)
                    last.then_inc(u_done, 1)

            attention_steps(pe, step)

            pe.wait_ge(totals, 1)
            pe.wait_ge(made_c, 1)
            pe.matmul(bank[7][:, 0:E], lower[:], upto[:, :, B - 1], start=True, stop=True)
            pe.matmul(bank[7][:, 8:8 + E], ones[:], upto[:, :, B - 1], start=True, stop=True).then_inc(counts, 1)

            def hot(q, r, first, last):
                n = q * HOT + r
                pe.wait_ge(hot_q_made, n + 1)
                pe.wait_ge(hot_coded[r % 2], q * (HOT // 2) + r // 2 + 1)
                pe.wait_ge(hot_scaled, n + 1)
                for g in range(QUAD):
                    mm = pe.matmul(bank[0][:, 0:2 * SLOTS], hot_q[r][:, :, g], hot_sv[:, r].rearrange("p a s g -> p (a s) g")[:, :, g],
                                   start=first and g == 0, stop=last and g == QUAD - 1)
                mm.then_inc(hot_used, 1)
            hot_steps(pe, hot)

            pe.wait_ge(experts_known, 1)
            pe.wait_ge(w_low, NB)
            pe.wait_ge(b_joined, 16)
            pe.wait_ge(found_copied, 1)

            expert_reg = [pe.alloc_register(f"expert{i}") for i in range(8)]

            def expert_at(r, k):
                return pe.snap(expert_reg[(r - k) % 8], min_val=0, max_val=E - 1)

            def step(q, r, has):
                if has(6):
                    j, e, turn = slot(q, r, 6)
                    pe.wait_ge(gelu_done, j + 1)
                    wait(pe, hT_low_done, j - 1)
                    for c in range(C):
                        last = pe.transpose(bank[4 + e % 2][:, c * P:(c + 1) * P], act_h[:, e % 2, c * P:(c + 1) * P], ident[:])
                    last.then_inc(hT_done, 1)
                if has(3):
                    j, e, turn = slot(q, r, 3)
                    pe.wait_ge(gathered[e], turn * 16 + 16)
                    wait(pe, gT_low, j - 1)
                    pe.transpose(bank[e % 2][:, 0:P], xg[e], ident[:]).then_inc(gT_done, 1)
                if has(4):
                    j, e, turn = slot(q, r, 4)
                    expert = expert_at(r, 4)
                    wait(pe, biased, j - 1)
                    pre = bank[2 + e % 2][:]
                    pe.wait_ge(gT_low, j + 1)
                    pe.matmul(pre, xg_hi[:, e % 2], w1_hi[:, bass.ds(expert, 1), :], start=True, stop=False)
                    pe.matmul(pre, xg_hi[:, e % 2], w1_lo[:, bass.ds(expert, 1), :], start=False, stop=False)
                    pe.matmul(pre, xg_lo[:, e % 2], w1_hi[:, bass.ds(expert, 1), :], start=False, stop=True).then_inc(pre_done, 1)
                if r % 4 == 3 and has(3):
                    j, e, turn = slot(q, r, 3)
                    pe.load(expert_reg[(r - 3) % 8:(r - 3) % 8 + 4], slot_expert[0:1, bass.ds(j, 4)])
                if has(7):
                    j, e, turn = slot(q, r, 7)
                    expert = expert_at(r, 7)
                    wait(pe, y_copied, j - 1)
                    y = bank[6 + e % 2]
                    pe.wait_ge(hT_low_done, j + 1)
                    for c in range(C):
                        pe.matmul(y[:, 0:2 * D], hT_hi[:, e % 2, c * P:(c + 1) * P],
                                  w2_hl[:, bass.ds(expert, 1), c, :, :], start=(c == 0), stop=False)
                        pe.matmul(y[:, 0:D], hT_lo[:, e % 2, c * P:(c + 1) * P],
                                  w2_hl[:, bass.ds(expert, 1), c, 0, :], start=False, stop=False)
                    pe.matmul(y[:, 0:D], ones_r[:], b2_hl[:, bass.ds(expert, 1), :], start=False, stop=True).then_inc(y_done, 1)
            slot_steps(pe, step)


_INS = ['x', 'adj', 'L0_gnn_W', 'L0_gnn_a', 'L0_ffn_Wg', 'L0_ffn_bg', 'L0_ffn_W1', 'L0_ffn_b1', 'L0_ffn_W2', 'L0_ffn_b2']


def kernel(**inputs):
    import numpy as _np
    import concourse.bacc as _bacc
    from concourse import mybir as _mybir
    from concourse.bass_utils import run_bass_kernel_spmd as _run

    nc = _bacc.Bacc("TRN2", target_bir_lowering=False, num_devices=1)
    arrays, args = {}, []
    for name in _INS:
        a = _np.ascontiguousarray(inputs[name])
        arrays[f"in_{name}_dram"] = a
        args.append(nc.dram_tensor(f"in_{name}_dram", a.shape, _mybir.dt.from_np(a.dtype), kind="ExternalInput").ap())
    shape = inputs['x'].shape
    args.append(nc.dram_tensor("out_0_dram", shape, _mybir.dt.float32, kind="ExternalOutput").ap())
    gat_moe(nc, *args)
    r = _run(nc, [arrays], core_ids=[0])
    return r.results[0]["out_0_dram"]
```
